# Optimizing a Trainium2 kernel written in Bass

```python
import numpy as np
import jax
import jax.numpy as jnp

def _softmax(x, axis=-1):
    return jax.nn.softmax(x, axis=axis)

def _gelu(x):
    return jax.nn.gelu(x, approximate=True)

def _silu(x):
    return jax.nn.silu(x)

def _sigmoid(x):
    return jax.nn.sigmoid(x)

def _layernorm(x, axis=-1, eps=1e-05):
    m = jnp.mean(x, axis=axis, keepdims=True)
    v = jnp.var(x, axis=axis, keepdims=True)
    return (x - m) / jnp.sqrt(v + eps)

def _scatter_add(tgt, idx, src, axis=0):
    return tgt.at[idx].add(src)

def _segment_sum(src, seg, n):
    return jax.ops.segment_sum(src, seg, n)
kernel_name = 'mk_gnn_preln_d4_gnn_r16_4f8170'

def setup_inputs(seed: int=0):
    np.random.seed(seed)
    _w = jnp.asarray

    def _rec_inputs():
        import jax
        import jax.numpy as jnp
        _gk = jax.random.key(seed)
        x = -0.0002117 + 1 * jax.random.normal(jax.random.fold_in(_gk, 1), (625, 512), jnp.float32)
        src = jax.random.randint(jax.random.fold_in(_gk, 2), (20000,), 0, 625, jnp.int32)
        dst = jax.random.randint(jax.random.fold_in(_gk, 3), (20000,), 0, 625, jnp.int32)
        _o = jnp.argsort(dst, stable=True)
        src = src[_o]
        dst = dst[_o]
        edge_attr_4 = 0.00171547 + 0.999346 * jax.random.normal(jax.random.fold_in(_gk, 12), (20000, 4), jnp.float32)
        edge_attr_64 = 0.000279952 + 1.00013 * jax.random.normal(jax.random.fold_in(_gk, 13), (20000, 64), jnp.float32)
        edge_attr_8 = 0.000126197 + 0.999763 * jax.random.normal(jax.random.fold_in(_gk, 14), (20000, 8), jnp.float32)
        edge_type_8 = jax.random.randint(jax.random.fold_in(_gk, 16), (20000,), 0, 8, jnp.int32)
        edge_weight = jax.random.uniform(jax.random.fold_in(_gk, 17), (20000,), jnp.float32, 0.0, 0.999998)
        return (x, src, dst, edge_attr_4, edge_attr_64, edge_attr_8, edge_type_8, edge_weight)
    x, src, dst, edge_attr_4, edge_attr_64, edge_attr_8, edge_type_8, edge_weight = _rec_inputs()

    def _L0_gnn_setup():
        import jax, jax.numpy as jnp
        import numpy as np
        N_NODES = 3125
        IN_CH = 512
        OUT_CH = 512
        N_EDGES = 50000
        key = jax.random.key(seed)
        k_x, k_e, k_w, k_b = jax.random.split(key, 4)
        x = jax.random.normal(k_x, (N_NODES, IN_CH), dtype=jnp.float32)
        edge_index = jax.random.randint(k_e, (2, N_EDGES), 0, N_NODES, dtype=jnp.int32)
        bound = 1.0 / np.sqrt(2 * IN_CH)
        W = jax.random.uniform(k_w, (OUT_CH, 2 * IN_CH), minval=-bound, maxval=bound, dtype=jnp.float32)
        b = jax.random.uniform(k_b, (OUT_CH,), minval=-bound, maxval=bound, dtype=jnp.float32)
        return {'x': x, 'edge_index': edge_index, 'W': W, 'b': b}
    _L0_gnn_all = _L0_gnn_setup()
    _L0_gnn_in = {k: v for k, v in _L0_gnn_all.items() if k in ('W', 'b')}
    del _L0_gnn_all

    def _L1_gnn_setup():
        import jax, jax.numpy as jnp
        import numpy as np
        N_NODES = 1250
        N_EDGES = 20000
        D = 512
        NUM_RELS = 8
        NUM_BASES = 4

        def _rel_graph_conv(h, src, dst, etypes, norm, basis, comp, bias, loop_w, apply_relu):
            n = h.shape[0]
            hb = jnp.einsum('nd,bdo->bno', h, basis)
            coef = comp[etypes]
            m = coef[:, 0, None] * hb[0][src]
            for b in range(1, basis.shape[0]):
                m = m + coef[:, b, None] * hb[b][src]
            m = m * norm[:, None]
            agg = jax.ops.segment_sum(m, dst, num_segments=n)
            out = agg + bias + h @ loop_w
            if apply_relu:
                out = jax.nn.relu(out)
            return out
        key = jax.random.key(seed)
        ks = jax.random.split(key, 16)
        inp = {'emb': jax.random.normal(ks[0], (N_NODES, D), dtype=jnp.float32), 'src': jax.random.randint(ks[1], (N_EDGES,), 0, N_NODES), 'dst': jax.random.randint(ks[2], (N_EDGES,), 0, N_NODES), 'etypes': jax.random.randint(ks[3], (N_EDGES,), 0, NUM_RELS), 'edge_norm': jax.random.uniform(ks[4], (N_EDGES,), dtype=jnp.float32)}
        s = 1.0 / np.sqrt(D)
        inp['basis0'] = jax.random.normal(ks[5], (NUM_BASES, D, D), dtype=jnp.float32) * s
        inp['comp0'] = jax.random.normal(ks[6], (NUM_RELS, NUM_BASES), dtype=jnp.float32)
        inp['bias0'] = jnp.zeros((D,), dtype=jnp.float32)
        inp['loop0'] = jax.random.normal(ks[7], (D, D), dtype=jnp.float32) * s
        inp['basis1'] = jax.random.normal(ks[8], (NUM_BASES, D, D), dtype=jnp.float32) * s
        inp['comp1'] = jax.random.normal(ks[9], (NUM_RELS, NUM_BASES), dtype=jnp.float32)
        inp['bias1'] = jnp.zeros((D,), dtype=jnp.float32)
        inp['loop1'] = jax.random.normal(ks[10], (D, D), dtype=jnp.float32) * s
        return inp
    _L1_gnn_all = _L1_gnn_setup()
    _L1_gnn_in = {k: v for k, v in _L1_gnn_all.items() if k in ('basis0', 'comp0', 'bias0', 'loop0', 'basis1', 'comp1', 'bias1', 'loop1')}
    del _L1_gnn_all

    def _L2_gnn_setup():
        import jax, jax.numpy as jnp
        import numpy as np
        MUL = 128
        N_NODES = 625
        N_EDGES = 10000
        R_BASIS = 8
        HIDDEN = 64
        W_NUMEL = 4 * MUL
        SQRT3 = 3.0 ** 0.5
        SILU_2MOM = 1.679177
        AVG_NUM_NEIGHBORS = 10.0

        def _lin_irreps(x0, x1, W0, W1):
            y0 = x0 @ W0 / jnp.sqrt(jnp.float32(W0.shape[0]))
            y1 = jnp.einsum('num,uv->nvm', x1, W1) / jnp.sqrt(jnp.float32(W1.shape[0]))
            return (y0, y1)

        def _forward(node_feats, edge_attrs, edge_feats, edge_index, W_up0, W_up1, W_mlp1, W_mlp2, W_mlp3, W_mlp4, W_out0, W_out1):
            num_nodes = node_feats.shape[0]
            sender, receiver = (edge_index[0], edge_index[1])
            x0 = node_feats[:, :MUL]
            x1 = node_feats[:, MUL:].reshape(num_nodes, MUL, 3)
            x0, x1 = _lin_irreps(x0, x1, W_up0, W_up1)
            h = edge_feats
            for W in (W_mlp1, W_mlp2, W_mlp3):
                h = SILU_2MOM * jax.nn.silu(h @ W / jnp.sqrt(jnp.float32(W.shape[0])))
            tpw = h @ W_mlp4 / jnp.sqrt(jnp.float32(W_mlp4.shape[0]))
            w1, w2, w3, w4 = jnp.split(tpw, 4, axis=-1)
            s0 = x0[sender]
            s1 = x1[sender]
            y0 = edge_attrs[:, 0:1]
            y1 = edge_attrs[:, 1:4]
            p1 = w1 * s0 * y0
            p2 = (w2 * s0)[:, :, None] * y1[:, None, :]
            p3 = w3[:, :, None] * s1 * y0[:, None, :]
            p4 = w4 * jnp.einsum('eum,em->eu', s1, y1) / SQRT3
            m0 = jnp.concatenate([p1, p4], axis=-1)
            m1 = jnp.concatenate([p2, p3], axis=1)
            msg0 = jax.ops.segment_sum(m0, receiver, num_segments=num_nodes)
            msg1 = jax.ops.segment_sum(m1, receiver, num_segments=num_nodes)
            o0, o1 = _lin_irreps(msg0, msg1, W_out0, W_out1)
            out = jnp.concatenate([o0, o1.reshape(num_nodes, 3 * MUL)], axis=-1)
            return out / AVG_NUM_NEIGHBORS
        key = jax.random.key(seed)
        ks = jax.random.split(key, 12)
        rn = lambda k, s: jax.random.normal(k, s, dtype=jnp.float32)
        return {'node_feats': rn(ks[0], (N_NODES, 4 * MUL)), 'edge_attrs': rn(ks[1], (N_EDGES, 4)), 'edge_feats': rn(ks[2], (N_EDGES, R_BASIS)), 'edge_index': jax.random.randint(ks[3], (2, N_EDGES), 0, N_NODES), 'W_up0': rn(ks[4], (MUL, MUL)), 'W_up1': rn(ks[5], (MUL, MUL)), 'W_mlp1': rn(ks[6], (R_BASIS, HIDDEN)), 'W_mlp2': rn(ks[7], (HIDDEN, HIDDEN)), 'W_mlp3': rn(ks[8], (HIDDEN, HIDDEN)), 'W_mlp4': rn(ks[9], (HIDDEN, W_NUMEL)), 'W_out0': rn(ks[10], (2 * MUL, MUL)), 'W_out1': rn(ks[11], (2 * MUL, MUL))}
    _L2_gnn_all = _L2_gnn_setup()
    _L2_gnn_in = {k: v for k, v in _L2_gnn_all.items() if k in ('W_up0', 'W_up1', 'W_mlp1', 'W_mlp2', 'W_mlp3', 'W_mlp4', 'W_out0', 'W_out1')}
    del _L2_gnn_all

    def _L3_gnn_setup():
        import jax, jax.numpy as jnp
        import numpy as np
        N_NODES = 1250
        N_EDGES = 20000
        HIDDEN = 512
        EDGE_DIM = 64
        LN_EPS = 1e-05

        def mish(x):
            return x * jnp.tanh(jax.nn.softplus(x))
        key = jax.random.key(seed)
        ks = jax.random.split(key, 8)
        s = lambda fan_in: 1.0 / np.sqrt(fan_in)
        return {'x': jax.random.normal(ks[0], (N_NODES, HIDDEN), dtype=jnp.float32), 'edge_index': jax.random.randint(ks[1], (2, N_EDGES), 0, N_NODES, dtype=jnp.int64), 'edge_attr': jax.random.normal(ks[2], (N_EDGES, EDGE_DIM), dtype=jnp.float32), 'W1': jax.random.normal(ks[3], (2 * HIDDEN + EDGE_DIM, HIDDEN), dtype=jnp.float32) * s(2 * HIDDEN + EDGE_DIM), 'b1': jnp.zeros((HIDDEN,), dtype=jnp.float32), 'W2': jax.random.normal(ks[4], (HIDDEN, HIDDEN), dtype=jnp.float32) * s(HIDDEN), 'b2': jnp.zeros((HIDDEN,), dtype=jnp.float32), 'W3': jax.random.normal(ks[5], (2 * HIDDEN, HIDDEN), dtype=jnp.float32) * s(2 * HIDDEN), 'b3': jnp.zeros((HIDDEN,), dtype=jnp.float32), 'W4': jax.random.normal(ks[6], (HIDDEN, HIDDEN), dtype=jnp.float32) * s(HIDDEN), 'b4': jnp.zeros((HIDDEN,), dtype=jnp.float32), 'gamma': jnp.ones((HIDDEN,), dtype=jnp.float32), 'beta': jnp.zeros((HIDDEN,), dtype=jnp.float32)}
    _L3_gnn_all = _L3_gnn_setup()
    _L3_gnn_in = {k: v for k, v in _L3_gnn_all.items() if k in ('W1', 'b1', 'W2', 'b2', 'W3', 'b3', 'W4', 'b4', 'gamma', 'beta')}
    del _L3_gnn_all
    return {'x': x, 'src': src, 'dst': dst, 'edge_attr_4': edge_attr_4, 'edge_attr_64': edge_attr_64, 'edge_attr_8': edge_attr_8, 'edge_type_8': edge_type_8, 'edge_weight': edge_weight, 'L0_gnn_W': _L0_gnn_in['W'], 'L0_gnn_b': _L0_gnn_in['b'], 'L1_gnn_basis0': _L1_gnn_in['basis0'], 'L1_gnn_comp0': _L1_gnn_in['comp0'], 'L1_gnn_bias0': _L1_gnn_in['bias0'], 'L1_gnn_loop0': _L1_gnn_in['loop0'], 'L1_gnn_basis1': _L1_gnn_in['basis1'], 'L1_gnn_comp1': _L1_gnn_in['comp1'], 'L1_gnn_bias1': _L1_gnn_in['bias1'], 'L1_gnn_loop1': _L1_gnn_in['loop1'], 'L2_gnn_W_up0': _L2_gnn_in['W_up0'], 'L2_gnn_W_up1': _L2_gnn_in['W_up1'], 'L2_gnn_W_mlp1': _L2_gnn_in['W_mlp1'], 'L2_gnn_W_mlp2': _L2_gnn_in['W_mlp2'], 'L2_gnn_W_mlp3': _L2_gnn_in['W_mlp3'], 'L2_gnn_W_mlp4': _L2_gnn_in['W_mlp4'], 'L2_gnn_W_out0': _L2_gnn_in['W_out0'], 'L2_gnn_W_out1': _L2_gnn_in['W_out1'], 'L3_gnn_W1': _L3_gnn_in['W1'], 'L3_gnn_b1': _L3_gnn_in['b1'], 'L3_gnn_W2': _L3_gnn_in['W2'], 'L3_gnn_b2': _L3_gnn_in['b2'], 'L3_gnn_W3': _L3_gnn_in['W3'], 'L3_gnn_b3': _L3_gnn_in['b3'], 'L3_gnn_W4': _L3_gnn_in['W4'], 'L3_gnn_b4': _L3_gnn_in['b4'], 'L3_gnn_gamma': _L3_gnn_in['gamma'], 'L3_gnn_beta': _L3_gnn_in['beta']}

def reference(x, src, dst, edge_attr_4, edge_attr_64, edge_attr_8, edge_type_8, edge_weight, L0_gnn_W, L0_gnn_b, L1_gnn_basis0, L1_gnn_comp0, L1_gnn_bias0, L1_gnn_loop0, L1_gnn_basis1, L1_gnn_comp1, L1_gnn_bias1, L1_gnn_loop1, L2_gnn_W_up0, L2_gnn_W_up1, L2_gnn_W_mlp1, L2_gnn_W_mlp2, L2_gnn_W_mlp3, L2_gnn_W_mlp4, L2_gnn_W_out0, L2_gnn_W_out1, L3_gnn_W1, L3_gnn_b1, L3_gnn_W2, L3_gnn_b2, L3_gnn_W3, L3_gnn_b3, L3_gnn_W4, L3_gnn_b4, L3_gnn_gamma, L3_gnn_beta):
    import jax
    import jax.numpy as jnp

    def _L0_gnn_ref(x, edge_index, W, b):
        import jax, jax.numpy as jnp
        import numpy as np
        N_NODES = 3125
        IN_CH = 512
        OUT_CH = 512
        N_EDGES = 50000
        src, dst = (edge_index[0], edge_index[1])
        src_feats = x[src]
        neighbor_sum = jax.ops.segment_sum(src_feats, dst, num_segments=x.shape[0])
        neighbor_count = jax.ops.segment_sum(jnp.ones((src.shape[0],), dtype=x.dtype), dst, num_segments=x.shape[0])
        neighbor_count = jnp.maximum(neighbor_count, 1.0)
        neighbor_mean = neighbor_sum / neighbor_count[:, None]
        h = jnp.concatenate([x, neighbor_mean], axis=-1)
        return h @ W.T + b

    def _L1_gnn_ref(emb, src, dst, etypes, edge_norm, basis0, comp0, bias0, loop0, basis1, comp1, bias1, loop1):
        import jax, jax.numpy as jnp
        import numpy as np
        N_NODES = 1250
        N_EDGES = 20000
        D = 512
        NUM_RELS = 8
        NUM_BASES = 4

        def _rel_graph_conv(h, src, dst, etypes, norm, basis, comp, bias, loop_w, apply_relu):
            n = h.shape[0]
            hb = jnp.einsum('nd,bdo->bno', h, basis)
            coef = comp[etypes]
            m = coef[:, 0, None] * hb[0][src]
            for b in range(1, basis.shape[0]):
                m = m + coef[:, b, None] * hb[b][src]
            m = m * norm[:, None]
            agg = jax.ops.segment_sum(m, dst, num_segments=n)
            out = agg + bias + h @ loop_w
            if apply_relu:
                out = jax.nn.relu(out)
            return out
        h = _rel_graph_conv(emb, src, dst, etypes, edge_norm, basis0, comp0, bias0, loop0, True)
        h = _rel_graph_conv(h, src, dst, etypes, edge_norm, basis1, comp1, bias1, loop1, False)
        return h

    def _L2_gnn_ref(node_feats, edge_attrs, edge_feats, edge_index, W_up0, W_up1, W_mlp1, W_mlp2, W_mlp3, W_mlp4, W_out0, W_out1):
        import jax, jax.numpy as jnp
        import numpy as np
        MUL = 128
        N_NODES = 625
        N_EDGES = 10000
        R_BASIS = 8
        HIDDEN = 64
        W_NUMEL = 4 * MUL
        SQRT3 = 3.0 ** 0.5
        SILU_2MOM = 1.679177
        AVG_NUM_NEIGHBORS = 10.0

        def _lin_irreps(x0, x1, W0, W1):
            y0 = x0 @ W0 / jnp.sqrt(jnp.float32(W0.shape[0]))
            y1 = jnp.einsum('num,uv->nvm', x1, W1) / jnp.sqrt(jnp.float32(W1.shape[0]))
            return (y0, y1)

        def _forward(node_feats, edge_attrs, edge_feats, edge_index, W_up0, W_up1, W_mlp1, W_mlp2, W_mlp3, W_mlp4, W_out0, W_out1):
            num_nodes = node_feats.shape[0]
            sender, receiver = (edge_index[0], edge_index[1])
            x0 = node_feats[:, :MUL]
            x1 = node_feats[:, MUL:].reshape(num_nodes, MUL, 3)
            x0, x1 = _lin_irreps(x0, x1, W_up0, W_up1)
            h = edge_feats
            for W in (W_mlp1, W_mlp2, W_mlp3):
                h = SILU_2MOM * jax.nn.silu(h @ W / jnp.sqrt(jnp.float32(W.shape[0])))
            tpw = h @ W_mlp4 / jnp.sqrt(jnp.float32(W_mlp4.shape[0]))
            w1, w2, w3, w4 = jnp.split(tpw, 4, axis=-1)
            s0 = x0[sender]
            s1 = x1[sender]
            y0 = edge_attrs[:, 0:1]
            y1 = edge_attrs[:, 1:4]
            p1 = w1 * s0 * y0
            p2 = (w2 * s0)[:, :, None] * y1[:, None, :]
            p3 = w3[:, :, None] * s1 * y0[:, None, :]
            p4 = w4 * jnp.einsum('eum,em->eu', s1, y1) / SQRT3
            m0 = jnp.concatenate([p1, p4], axis=-1)
            m1 = jnp.concatenate([p2, p3], axis=1)
            msg0 = jax.ops.segment_sum(m0, receiver, num_segments=num_nodes)
            msg1 = jax.ops.segment_sum(m1, receiver, num_segments=num_nodes)
            o0, o1 = _lin_irreps(msg0, msg1, W_out0, W_out1)
            out = jnp.concatenate([o0, o1.reshape(num_nodes, 3 * MUL)], axis=-1)
            return out / AVG_NUM_NEIGHBORS
        return _forward(node_feats, edge_attrs, edge_feats, edge_index, W_up0, W_up1, W_mlp1, W_mlp2, W_mlp3, W_mlp4, W_out0, W_out1)

    def _L3_gnn_ref(x, edge_index, edge_attr, W1, b1, W2, b2, W3, b3, W4, b4, gamma, beta):
        import jax, jax.numpy as jnp
        import numpy as np
        N_NODES = 1250
        N_EDGES = 20000
        HIDDEN = 512
        EDGE_DIM = 64
        LN_EPS = 1e-05

        def mish(x):
            return x * jnp.tanh(jax.nn.softplus(x))
        src, dst = (edge_index[0], edge_index[1])
        edge_feat = jnp.concatenate([x[src], x[dst], edge_attr], axis=-1)
        h = mish(edge_feat @ W1 + b1)
        messages = mish(h @ W2 + b2)
        agg = jax.ops.segment_sum(messages, dst, num_segments=x.shape[0])
        u = mish(jnp.concatenate([x, agg], axis=-1) @ W3 + b3)
        out = u @ W4 + b4
        y = x + out
        mu = jnp.mean(y, axis=-1, keepdims=True)
        var = jnp.mean(jnp.square(y - mu), axis=-1, keepdims=True)
        return (y - mu) * jax.lax.rsqrt(var + LN_EPS) * gamma + beta
    edge_index = jnp.stack([src, dst])
    h = jnp.maximum(_layernorm(x, axis=-1), 0.0)
    x = x + _L0_gnn_ref(h, edge_index, L0_gnn_W, L0_gnn_b)
    h = jnp.maximum(_layernorm(x, axis=-1), 0.0)
    x = x + _L1_gnn_ref(h, src, dst, edge_type_8, edge_weight, L1_gnn_basis0, L1_gnn_comp0, L1_gnn_bias0, L1_gnn_loop0, L1_gnn_basis1, L1_gnn_comp1, L1_gnn_bias1, L1_gnn_loop1)
    h = jnp.maximum(_layernorm(x, axis=-1), 0.0)
    x = x + _L2_gnn_ref(h, edge_attr_4, edge_attr_8, edge_index, L2_gnn_W_up0, L2_gnn_W_up1, L2_gnn_W_mlp1, L2_gnn_W_mlp2, L2_gnn_W_mlp3, L2_gnn_W_mlp4, L2_gnn_W_out0, L2_gnn_W_out1)
    h = jnp.maximum(_layernorm(x, axis=-1), 0.0)
    x = x + _L3_gnn_ref(h, edge_index, edge_attr_64, L3_gnn_W1, L3_gnn_b1, L3_gnn_W2, L3_gnn_b2, L3_gnn_W3, L3_gnn_b3, L3_gnn_W4, L3_gnn_b4, L3_gnn_gamma, L3_gnn_beta)
    return x

_drawn_inputs = setup_inputs


def setup_inputs(seed=0):
    import zlib

    import numpy as np

    out = dict(_drawn_inputs(seed))
    spreads = {'L1_gnn_bias0': (0.0, 0.1),
     'L1_gnn_bias1': (0.0, 0.1),
     'L3_gnn_b1': (0.0, 0.1),
     'L3_gnn_b2': (0.0, 0.1),
     'L3_gnn_b3': (0.0, 0.1),
     'L3_gnn_b4': (0.0, 0.1),
     'L3_gnn_gamma': (1.0, 0.2),
     'L3_gnn_beta': (0.0, 0.1)}
    factors = {}
    for name, (base, spread) in spreads.items():
        noise = np.random.default_rng([zlib.crc32(name.encode()), seed]).standard_normal(out[name].shape)
        drawn = base * np.exp(spread * noise) if base else spread * noise
        out[name] = jnp.asarray(drawn.astype(out[name].dtype))
    for name, factor in factors.items():
        out[name] = (out[name] * factor).astype(out[name].dtype)
    return out
```

```python
import numpy as np
import concourse.bass as bass
from concourse import mybir
from contextlib import ExitStack

FP32 = mybir.dt.float32
I32 = mybir.dt.int32
U32 = mybir.dt.uint32
ALU = mybir.AluOpType
ACT = mybir.ActivationFunctionType

P = 128
NODES, D, EDGES = 625, 512, 20000
NB, BN = 5, 125
EP = 125
EC = EDGES // EP
TG = 4
SG = TG * P
NG = (EDGES + NB * (SG - 1)) // SG
NG += NG % 2
NT = NG * TG
RECORD = 80
A64, A8, SMALL, SRC, DST, TYPE = 0, 64, 72, 77, 78, 79
Y, WEIGHT = 0, 4
RELS, BASES = 8, 4
MUL, HID = 128, 64
SILU_2MOM = 1.679177
EPS = 1e-5


class Program:

    def __init__(self, nc, args, out):
        self.nc, self.inp, self.out = nc, args, out
        self.keep = ExitStack()

    def sb(self, name, shape, dt=FP32, ctx=None):
        return (ctx or self.keep).enter_context(self.nc.sbuf_tensor(name, shape, dt))


def constants(pg):
    nc = pg.nc
    pg.iota_free = pg.sb("iota_free", [P, NT])
    pg.ident = pg.sb("ident", [P, P])
    pg.ones = pg.sb("ones", [P, P])
    pg.before = pg.sb("before", [P, P])
    pg.minus_half = pg.sb("minus_half", [P, 1])
    pg.passes = 0
    pg.arrived = [pg.keep.enter_context(nc.semaphore(f"arrived{b}")) for b in range(2 * TG)]
    with nc.semaphore("filled") as filled, nc.Block() as block:

        @block.gpsimd
        def _(pool):
            nc.gpsimd.iota(pg.iota_free[:, :], [[1, NT]], base=0, channel_multiplier=0,
                           allow_small_or_imprecise_dtypes=True)
            nc.gpsimd.memset(pg.minus_half[:, :], -0.5)
            nc.gpsimd.memset(pg.ident[:, :], 0.0).then_inc(filled, 1)
            nc.gpsimd.memset(pg.ones[:, :], 1.0).then_inc(filled, 1)
            pool.wait_ge(filled, 2)
            nc.gpsimd.affine_select(out=pg.ident[:, :], in_=pg.ident[:, :], compare_op=ALU.not_equal, fill=1.0,
                                    base=0, pattern=[[-1, P]], channel_multiplier=1)
            nc.gpsimd.affine_select(out=pg.before[:, :], in_=pg.ones[:, :], compare_op=ALU.is_gt, fill=0.0,
                                    base=0, pattern=[[1, P]], channel_multiplier=-1)


def place_edges(pg):
    nc = pg.nc
    ctx = ExitStack()
    pg.lane = pg.sb("lane", [EP, EC])
    pg.tile = pg.sb("tile", [EP, EC])
    pg.edge1 = pg.sb("edge1", [EP, EC])
    pg.block_of_tile = pg.sb("block_of_tile", [P, NT])
    pg.block_of_group = pg.sb("block_of_group", [1, NG], I32)
    pg.records = nc.dram_tensor("records", [EDGES, RECORD], FP32).ap()
    with ctx, ExitStack() as psums:
        dst_i = pg.sb("dst_i", [EP, EC], I32, ctx)
        dst = pg.sb("dst", [EP, EC], ctx=ctx)
        block_of = pg.sb("block_of", [EP, EC], ctx=ctx)
        over = pg.sb("over", [EP, EC], ctx=ctx)
        zero = pg.sb("zero", [EP, EC], ctx=ctx)
        mine = pg.sb("mine", [EP, NB, EC], ctx=ctx)
        rank = pg.sb("rank", [EP, NB, EC], ctx=ctx)
        in_row = pg.sb("in_row", [EP, NB], ctx=ctx)
        total = pg.sb("total", [P, NB], ctx=ctx)
        group_edge = pg.sb("group_edge", [P, 40], ctx=ctx)
        full = pg.sb("full", [P, 40], ctx=ctx)
        groups = pg.sb("groups", [P, NB], ctx=ctx)
        first_group = pg.sb("first_group", [P, NB + 1], ctx=ctx)
        shift = pg.sb("shift", [EP, NB], ctx=ctx)
        slot = pg.sb("slot", [EP, EC], ctx=ctx)
        slot_i = pg.sb("slot_i", [EP, EC], I32, ctx)
        lane_i = pg.sb("lane_i", [EP, EC], I32, ctx)
        tile_i = pg.sb("tile_i", [EP, EC], I32, ctx)
        group_no = pg.sb("group_no", [P, NG], ctx=ctx)
        group_blk = pg.sb("group_blk", [P, NG], ctx=ctx)
        record = pg.sb("record", [EP, EC, RECORD], ctx=ctx)
        ints = pg.sb("ints", [EP, 3, EC], I32, ctx)
        row_ps = psums.enter_context(nc.psum_tensor("row_ps", [P, 512], FP32))
        sem = {n: psums.enter_context(nc.semaphore(n)) for n in
               ("dst_in", "record_in", "ints_in", "iota_done", "chain", "rows_counted", "rows_summed",
                "record_built", "record_out")}
        block = psums.enter_context(nc.Block())

        @block.sync
        def _(sp):
            sp.dma_start(dst_i[:, :], pg.inp["dst"].rearrange("(p j) -> p j", j=EC)).then_inc(sem["dst_in"], 16)
            sp.dma_start(record[:, :, :].rearrange("p j r -> p (j r)"),
                         pg.inp["edge_floats"].rearrange("(p j) r -> p (j r)", j=EC)).then_inc(sem["record_in"], 16)
            for n, name in enumerate(("src", "dst", "edge_type_8")):
                sp.dma_start(ints[:, n, :], pg.inp[name].rearrange("(p j) -> p j", j=EC)).then_inc(sem["ints_in"], 16)
            sp.wait_ge(sem["record_built"], 3)
            sp.dma_start(pg.records.rearrange("(p j) r -> p (j r)", j=EC),
                         record[:, :, :].rearrange("p j r -> p (j r)")).then_inc(sem["record_out"], 16)
            sp.wait_ge(sem["record_out"], 16)

        @block.gpsimd
        def _(pool):
            nc.gpsimd.iota(group_edge[:, :], [[SG, 40]], base=0, channel_multiplier=0,
                           allow_small_or_imprecise_dtypes=True)
            nc.gpsimd.iota(group_no[:, :], [[1, NG]], base=0, channel_multiplier=0,
                           allow_small_or_imprecise_dtypes=True)
            nc.gpsimd.iota(pg.edge1[:, :], [[1, EC]], base=1, channel_multiplier=EC,
                           allow_small_or_imprecise_dtypes=True).then_inc(sem["iota_done"], 1)

        @block.scalar
        def _(act):
            act.wait_ge(sem["ints_in"], 48)
            act.wait_ge(sem["record_in"], 16)
            for n, at in enumerate((SRC, DST, TYPE)):
                nc.scalar.copy(record[:, :, at], ints[:, n, :]).then_inc(sem["record_built"], 1)

        @block.tensor
        def _(pe):
            pe.wait_ge(sem["rows_counted"], 1)
            nc.tensor.matmul(row_ps[0:EP, 0:NB], pg.before[0:EP, 0:EP], in_row[:, :], start=True, stop=True)
            nc.tensor.matmul(row_ps[:, 8:8 + NB], pg.ones[0:EP, :], in_row[:, :],
                             start=True, stop=True).then_inc(sem["rows_summed"], 1)

        @block.vector
        def _(dve):
            done = [0]

            def link(ins):
                done[0] += 1
                ins.then_inc(sem["chain"], 1)
                dve.wait_ge(sem["chain"], done[0])

            nc.vector.memset(zero[:, :], 0.0)
            dve.wait_ge(sem["dst_in"], 16)
            link(nc.vector.tensor_copy(dst[:, :], dst_i[:, :]))
            link(nc.vector.tensor_scalar(block_of[:, :], dst[:, :], float(BN), None, ALU.is_ge))
            for b in range(2, NB):
                link(nc.vector.scalar_tensor_tensor(out=block_of[:, :], in0=dst[:, :], scalar=float(BN * b),
                                                    in1=block_of[:, :], op0=ALU.is_ge, op1=ALU.add))
            for b in range(NB):
                last = nc.vector.tensor_scalar(mine[:, b, :], block_of[:, :], float(b), None, ALU.is_equal)
            link(last)
            for b in range(NB):
                last = nc.vector.tensor_tensor_scan(out=rank[:, b, :], data0=mine[:, b, :], data1=zero[:, :],
                                                    initial=0.0, op0=ALU.add, op1=ALU.add)
            link(last)
            nc.vector.tensor_copy(in_row[:, :], rank[:, :, EC - 1]).then_inc(sem["rows_counted"], 1)
            dve.wait_ge(sem["rows_summed"], 1)
            dve.wait_ge(sem["iota_done"], 1)
            link(nc.vector.tensor_copy(total[:, :], row_ps[:, 8:8 + NB]))
            for b in range(NB):
                link(nc.vector.tensor_scalar(full[:, :], group_edge[:, :], total[:, b:b + 1], 0.0, ALU.is_lt,
                                             ALU.add, accum_out=groups[:, b:b + 1]))
            link(nc.vector.memset(first_group[:, 0:1], 0.0))
            for b in range(NB):
                link(nc.vector.tensor_tensor(first_group[:, b + 1:b + 2], first_group[:, b:b + 1],
                                             groups[:, b:b + 1], ALU.add))
            link(nc.vector.tensor_scalar(group_blk[:, :], group_no[:, :], first_group[:, 1:2], None, ALU.is_ge))
            for b in range(2, NB):
                link(nc.vector.scalar_tensor_tensor(out=group_blk[:, :], in0=group_no[:, :],
                                                    scalar=first_group[:, b:b + 1], in1=group_blk[:, :],
                                                    op0=ALU.is_ge, op1=ALU.add))
            nc.vector.tensor_copy(pg.block_of_group[:, :], group_blk[0:1, :])
            for k in range(TG):
                nc.vector.tensor_copy(pg.block_of_tile[:, :].rearrange("p (g k) -> p g k", k=TG)[:, :, k],
                                      group_blk[:, :])
            link(nc.vector.scalar_tensor_tensor(out=shift[:, :], in0=first_group[0:EP, 0:NB], scalar=float(SG),
                                                in1=row_ps[0:EP, 0:NB], op0=ALU.mult, op1=ALU.add))
            for b in range(NB):
                last = nc.vector.scalar_tensor_tensor(out=rank[:, b, :], in0=rank[:, b, :], scalar=shift[:, b:b + 1],
                                                      in1=mine[:, b, :], op0=ALU.add, op1=ALU.mult)
            link(last)
            link(nc.vector.tensor_scalar(slot[:, :], rank[:, 0, :], 1.0, None, ALU.subtract))
            for b in range(1, NB):
                link(nc.vector.tensor_tensor(slot[:, :], slot[:, :], rank[:, b, :], ALU.add))
            link(nc.vector.tensor_copy(slot_i[:, :], slot[:, :]))
            nc.vector.tensor_scalar(lane_i[:, :], slot_i[:, :], P - 1, None, ALU.bitwise_and)
            link(nc.vector.tensor_scalar(tile_i[:, :], slot_i[:, :], 7, None, ALU.arith_shift_right))
            nc.vector.tensor_copy(pg.lane[:, :], lane_i[:, :])
            nc.vector.tensor_copy(pg.tile[:, :], tile_i[:, :])


def order_edges(pg):
    nc = pg.nc
    pg.edge_no = pg.sb("edge_no", [P, NT], U32)
    pg.filled = pg.sb("filled", [P, NT])
    with ExitStack() as ctx:
        lane_hot = pg.sb("lane_hot", [EP, 2, P], ctx=ctx)
        tile_edge = pg.sb("tile_edge", [EP, 2, NT], ctx=ctx)
        edge_f = pg.sb("edge_f", [P, NT], ctx=ctx)
        slots_ps = ctx.enter_context(nc.psum_tensor("slots_ps", [P, 512], FP32))
        hot, free, zeroed, placed, edge_sem = (ctx.enter_context(nc.semaphore(n)) for n in
                                       ("hot_ready", "hot_free", "slots_zeroed", "placed", "edge_chain"))
        block = ctx.enter_context(nc.Block())

        @block.vector
        def _(dve):
            with dve.Fori(0, EC // 2) as i:
                for s in range(2):
                    dve.wait_ge(free, 2 * i + s + 1)
                    j = 2 * i + s
                    nc.vector.tensor_scalar(lane_hot[:, s, :], pg.iota_free[0:EP, 0:P], pg.lane[:, bass.ds(j, 1)],
                                            None, ALU.is_equal)
                    nc.vector.tensor_scalar(tile_edge[:, s, :], pg.iota_free[0:EP, :], pg.tile[:, bass.ds(j, 1)],
                                            pg.edge1[:, bass.ds(j, 1)], ALU.is_equal, ALU.mult).then_inc(hot, 1)
            dve.wait_ge(placed, 1)
            nc.vector.tensor_scalar(pg.filled[:, :], slots_ps[:, 0:NT], 0.0, None, ALU.is_gt)
            nc.vector.tensor_scalar(edge_f[:, :], slots_ps[:, 0:NT], -1.0, 0.0, ALU.add, ALU.max).then_inc(edge_sem, 1)
            dve.wait_ge(edge_sem, 1)
            nc.vector.tensor_copy(pg.edge_no[:, :], edge_f[:, :])

        @block.gpsimd
        def _(pool):
            nc.gpsimd.memset(edge_f[:, :], 0.0).then_inc(zeroed, 1)

        @block.tensor
        def _(pe):
            pe.sem_inc(free, 2)
            pe.wait_ge(zeroed, 1)
            nc.tensor.matmul(slots_ps[:, 0:NT], pg.ident[:, :], edge_f[:, :], start=True, stop=False)
            with pe.Fori(0, EC // 2) as i:
                for s in range(2):
                    pe.wait_ge(hot, 2 * i + s + 1)
                    nc.tensor.matmul(slots_ps[:, 0:NT], lane_hot[:, s, :], tile_edge[:, s, :],
                                     start=False, stop=False).then_inc(free, 1)
            nc.tensor.matmul(slots_ps[:, 0:NT], pg.ident[:, :], edge_f[:, :], start=False, stop=True).then_inc(placed, 1)


def gather_loop(pg, pool, sems, table, rows, buffers, idx_tiles, width):
    nc = pg.nc
    passed = sems["passed"]
    idx_copied, free, arrived = sems["idx_copied"], sems["gather_free"], sems["arrived"]
    with pool.Fori(0, NG // 2) as i:
        for h in range(2):
            pool.wait_ge(free, (2 * i + h + 1) * TG)
            pool.sem_inc(passed, 1)
            nc.gpsimd.tensor_copy(idx_tiles[:, h, :], rows[:, bass.ds((2 * i + h) * TG, TG)]).then_inc(idx_copied, 1)
            pool.wait_ge(idx_copied, 2 * i + h + 1)
            pool.sem_inc(passed, 1)
            for k in range(TG):
                b = h * TG + k
                nc.gpsimd.indirect_dma_start(
                    out=buffers[:, b, 0:width], out_offset=None, in_=table,
                    in_offset=bass.IndirectOffsetOnAxis(ap=idx_tiles[:, h, k:k + 1], axis=0)).then_inc(arrived[b], 16)


def gather_sems(pg, ctx, tag):
    nc = pg.nc
    sems = {n: ctx.enter_context(nc.semaphore(f"{tag}_{n}")) for n in ("idx_copied", "gather_free", "passed")}
    sems["arrived"] = pg.arrived
    sems["before"] = pg.passes * 16 * (NG // 2)
    pg.passes += 1
    return sems


def fetch_records(pg):
    nc = pg.nc
    REST = RECORD - SMALL
    pg.record = pg.sb("slot_record", [P, NT, REST])
    pg.src_row = pg.sb("src_row", [P, NT], U32)
    pg.rel_row = pg.sb("rel_row", [P, NT], U32)
    pg.dst_in_block = pg.sb("dst_in_block", [P, NT])
    pg.attrT = nc.dram_tensor("attrT", [NG, SMALL, SG], FP32).ap()
    with ExitStack() as ctx:
        landing = pg.sb("landing", [P, 2 * TG, RECORD], ctx=ctx)
        idx = pg.sb("idx", [P, 2, TG], U32, ctx)
        turned = pg.sb("attr_rows", [SMALL, 2, SG], ctx=ctx)
        t0 = pg.sb("t0", [P, NT], ctx=ctx)
        t1 = pg.sb("t1", [P, NT], ctx=ctx)
        ps = [ctx.enter_context(nc.psum_tensor(f"rec_ps{h}", [P, SG], FP32)) for h in range(2)]
        sems = gather_sems(pg, ctx, "rec")
        chain, kept, made, copied = (ctx.enter_context(nc.semaphore(n)) for n in
                                     ("rec_chain", "rec_kept", "rec_made", "rec_copied"))
        stored = [ctx.enter_context(nc.semaphore(f"rec_stored{h}")) for h in range(2)]
        block = ctx.enter_context(nc.Block())

        @block.gpsimd
        def _(pool):
            gather_loop(pg, pool, sems, pg.records, pg.edge_no, landing, idx, RECORD)

        @block.tensor
        def _(pe):
            pe.sem_inc(sems["gather_free"], 2 * TG)
            pe.sem_inc(copied, 2)
            with pe.Fori(0, NG // 2) as i:
                for h in range(2):
                    pe.wait_ge(copied, 2 * i + h + 1)
                    for k in range(TG):
                        pe.wait_ge(sems["arrived"][h * TG + k], sems["before"] + 16 * i + 16)
                        nc.tensor.transpose(ps[h][0:SMALL, k * P:(k + 1) * P], landing[:, h * TG + k, 0:SMALL],
                                            pg.ident[:, :]).then_inc(made, 1)
                    pe.wait_ge(made, (2 * i + h + 1) * TG)
                    pe.wait_ge(kept, (2 * i + h + 1) * TG)
                    pe.sem_inc(sems["gather_free"], TG)

        @block.scalar
        def _(act):
            act.sem_inc(stored[0], 16)
            act.sem_inc(stored[1], 16)
            with act.Fori(0, NG // 2) as i:
                for h in range(2):
                    act.wait_ge(stored[h], 16 * i + 16)
                    act.wait_ge(made, (2 * i + h + 1) * TG)
                    nc.scalar.copy(turned[:, h, :], ps[h][0:SMALL, :]).then_inc(copied, 1)

        @block.sync
        def _(sp):
            with sp.Fori(0, NG // 2) as i:
                for h in range(2):
                    sp.wait_ge(copied, 2 * i + h + 3)
                    sp.dma_start(pg.attrT[bass.ds(2 * i + h, 1), :, :].rearrange("a r e -> (a r) e"),
                                 turned[:, h, :]).then_inc(stored[h], 16)
            for h in range(2):
                sp.wait_ge(stored[h], 16 * (NG // 2) + 16)

        @block.vector
        def _(dve):
            done = [0]

            def link(ins):
                done[0] += 1
                ins.then_inc(chain, 1)
                dve.wait_ge(chain, done[0])

            with dve.Fori(0, NG // 2) as i:
                for b in range(2 * TG):
                    dve.wait_ge(sems["arrived"][b], sems["before"] + 16 * i + 16)
                    nc.vector.tensor_copy(pg.record[:, bass.ds(i * 2 * TG + b, 1), :].rearrange("p a r -> p (a r)"),
                                          landing[:, b, SMALL:RECORD]).then_inc(kept, 1)
            dve.wait_ge(kept, NT)
            src, dst, rel = (pg.record[:, :, at - SMALL] for at in (SRC, DST, TYPE))
            nc.vector.tensor_copy(pg.src_row[:, :], src)
            link(nc.vector.scalar_tensor_tensor(out=t0[:, :], in0=rel, scalar=float(NODES),
                                                in1=src, op0=ALU.mult, op1=ALU.add))
            nc.vector.tensor_copy(pg.rel_row[:, :], t0[:, :])
            link(nc.vector.scalar_tensor_tensor(out=t1[:, :], in0=pg.block_of_tile[:, :], scalar=-float(BN),
                                                in1=dst, op0=ALU.mult, op1=ALU.add))
            link(nc.vector.scalar_tensor_tensor(out=t1[:, :], in0=t1[:, :], scalar=1.0, in1=pg.filled[:, :],
                                                op0=ALU.add, op1=ALU.mult))
            nc.vector.tensor_scalar(pg.dst_in_block[:, :], t1[:, :], -1.0, None, ALU.add)


def load_nodes(pg):
    nc = pg.nc
    pg.x = pg.sb("x", [BN, NB, D])
    pg.h = pg.sb("h", [BN, NB, D])
    pg.hT = pg.sb("hT", [P, D // P, NODES])
    with nc.semaphore("x_in") as x_in, nc.Block() as block:
        @block.sync
        def _(sp):
            sp.dma_start(pg.x[:, :, :], pg.inp["x"].rearrange("(b p) d -> p b d", p=BN)).then_inc(x_in, 16)
            sp.wait_ge(x_in, 16)


def normalize(pg, tag, h_table=None):
    nc = pg.nc
    with ExitStack() as ctx:
        stats = pg.sb(f"{tag}_stats", [BN, NB, 6], ctx=ctx)
        mv = pg.sb(f"{tag}_mv", [BN, NB, 2], ctx=ctx)
        sd = pg.sb(f"{tag}_sd", [BN, NB], ctx=ctx)
        rs = pg.sb(f"{tag}_rs", [BN, NB], ctx=ctx)
        nmr = pg.sb(f"{tag}_nmr", [BN, NB], ctx=ctx)
        ps = [ctx.enter_context(nc.psum_tensor(f"{tag}_ps{i}", [P, D // P, P], FP32)) for i in range(2)]
        chain, var, root, scaled, normed, turned, taken, stored = (
            ctx.enter_context(nc.semaphore(f"{tag}_{n}"))
            for n in ("chain", "var", "root", "scaled", "normed", "turned", "taken", "stored"))
        block = ctx.enter_context(nc.Block())

        @block.vector
        def _(dve):
            for b in range(NB):
                last = nc.vector.bn_stats(out=stats[:, b, :], in_=pg.x[:, b, :])
            last.then_inc(chain, 1)
            dve.wait_ge(chain, 1)
            for b in range(NB):
                last = nc.vector.bn_aggr(out=mv[:, b, :], in_=stats[:, b, :])
            last.then_inc(chain, 1)
            dve.wait_ge(chain, 2)
            nc.vector.tensor_scalar(sd[:, :], mv[:, :, 1], EPS, None, ALU.add).then_inc(var, 1)
            dve.wait_ge(root, 1)
            nc.vector.reciprocal(rs[:, :], sd[:, :]).then_inc(chain, 1)
            dve.wait_ge(chain, 3)
            nc.vector.scalar_tensor_tensor(out=nmr[:, :], in0=mv[:, :, 0], scalar=-1.0, in1=rs[:, :],
                                           op0=ALU.mult, op1=ALU.mult).then_inc(scaled, 1)
            for b in range(NB):
                dve.wait_ge(turned, b + 1)
                nc.vector.tensor_copy(pg.hT[:, :, b * BN:(b + 1) * BN], ps[b % 2][:, :, 0:BN]).then_inc(taken, 1)

        @block.scalar
        def _(act):
            act.wait_ge(var, 1)
            nc.scalar.sqrt(sd[:, :], sd[:, :]).then_inc(root, 1)
            act.wait_ge(scaled, 1)
            for b in range(NB):
                nc.scalar.activation(pg.h[:, b, :], pg.x[:, b, :], ACT.Relu, bias=nmr[:, b:b + 1],
                                     scale=rs[:, b:b + 1]).then_inc(normed, 1)

        @block.sync
        def _(sp):
            if h_table is not None:
                sp.wait_ge(normed, NB)
                sp.dma_start(h_table.rearrange("(b p) d -> p b d", p=BN), pg.h[:, :, :]).then_inc(stored, 16)
                sp.wait_ge(stored, 16)

        @block.tensor
        def _(pe):
            for b in range(NB):
                pe.wait_ge(normed, b + 1)
                if b >= 2:
                    pe.wait_ge(taken, b - 1)
                for f in range(D // P):
                    last = nc.tensor.transpose(ps[b % 2][:, f, 0:BN], pg.h[:, b, f * P:(f + 1) * P],
                                               pg.ident[0:BN, 0:BN])
                last.then_inc(turned, 1)


def transpose_nodes(pg, tag, src, dst, blocks_of_columns):
    nc = pg.nc
    with ExitStack() as ctx:
        ps = [ctx.enter_context(nc.psum_tensor(f"{tag}_ps{i}", [P, 4, P], FP32)) for i in range(2)]
        turned, taken = (ctx.enter_context(nc.semaphore(f"{tag}_{n}")) for n in ("turned", "taken"))
        block = ctx.enter_context(nc.Block())
        steps = [(b, f0) for b in range(NB) for f0 in range(0, blocks_of_columns, 4)]

        @block.tensor
        def _(pe):
            for n, (b, f0) in enumerate(steps):
                if n >= 2:
                    pe.wait_ge(taken, n - 1)
                for f in range(4):
                    last = nc.tensor.transpose(ps[n % 2][:, f, 0:BN], src[:, b, (f0 + f) * P:(f0 + f + 1) * P],
                                               pg.ident[0:BN, 0:BN])
                last.then_inc(turned, 1)

        @block.vector
        def _(dve):
            for n, (b, f0) in enumerate(steps):
                dve.wait_ge(turned, n + 1)
                nc.vector.tensor_copy(dst[:, f0:f0 + 4, b * BN:(b + 1) * BN], ps[n % 2][:, :, 0:BN]).then_inc(taken, 1)


def segment_sum(pg, tag, table, rows, total, weight=None, count=None):
    nc = pg.nc
    with ExitStack() as ctx:
        got = pg.sb(f"{tag}_got", [P, 2 * TG, D], ctx=ctx)
        idx = pg.sb(f"{tag}_idx", [P, 2, TG], U32, ctx)
        hot = pg.sb(f"{tag}_hot", [P, 2 * TG, BN], ctx=ctx)
        sum_ps = [ctx.enter_context(nc.psum_tensor(f"{tag}_sum{h}", [P, D], FP32)) for h in range(2)]
        cnt_ps = [ctx.enter_context(nc.psum_tensor(f"{tag}_cnt{h}", [P, D], FP32)) for h in range(2)]
        sems = gather_sems(pg, ctx, tag)
        hot_ready, hot_free, summed, added, cleared = (
            ctx.enter_context(nc.semaphore(f"{tag}_{n}"))
            for n in ("hot_ready", "hot_free", "summed", "added", "cleared"))
        block = ctx.enter_context(nc.Block())

        @block.gpsimd
        def _(pool):
            nc.gpsimd.memset(total[:, :, :], 0.0).then_inc(cleared, 1)
            if count is not None:
                nc.gpsimd.memset(count[:, :], 0.0).then_inc(cleared, 1)
            gather_loop(pg, pool, sems, table, rows, got, idx, D)

        @block.tensor
        def _(pe):
            pe.sem_inc(sems["gather_free"], 2 * TG)
            pe.sem_inc(hot_free, 2 * TG)
            with pe.Fori(0, NG // 2) as i:
                for h in range(2):
                    pe.wait_ge(added, 2 * i + h + 1)
                    for k in range(TG):
                        b = h * TG + k
                        pe.wait_ge(sems["arrived"][b], sems["before"] + 16 * i + 16)
                        pe.wait_ge(hot_ready, (2 * i + h) * TG + k + 1)
                        if count is not None:
                            nc.tensor.matmul(cnt_ps[h][0:BN, 0:1], hot[:, b, :], pg.ones[:, 0:1],
                                             start=(k == 0), stop=(k == TG - 1))
                        last = nc.tensor.matmul(sum_ps[h][0:BN, :], hot[:, b, :], got[:, b, :],
                                                start=(k == 0), stop=(k == TG - 1))
                        last.then_inc(hot_free, 1)
                    pe.wait_ge(hot_free, (2 * i + h + 1) * TG + 2 * TG)
                    pe.sem_inc(sems["gather_free"], TG)
                    pe.sem_inc(summed, 1)

        @block.vector
        def _(dve):
            dve.sem_inc(added, 2)
            dve.wait_ge(cleared, 1 if count is None else 2)
            with dve.Fori(0, NG // 2) as i:
                for h in range(2):
                    for k in range(TG):
                        b, t = h * TG + k, (2 * i + h) * TG + k
                        dve.wait_ge(hot_free, t + 1)
                        if weight is None:
                            nc.vector.tensor_scalar(hot[:, b, :], pg.iota_free[:, 0:BN],
                                                    pg.dst_in_block[:, bass.ds(t, 1)], None,
                                                    ALU.is_equal).then_inc(hot_ready, 1)
                        else:
                            nc.vector.tensor_scalar(hot[:, b, :], pg.iota_free[:, 0:BN],
                                                    pg.dst_in_block[:, bass.ds(t, 1)], weight(t),
                                                    ALU.is_equal, ALU.mult).then_inc(hot_ready, 1)
                for h in range(2):
                    at = nc.vector.value_load(pg.block_of_group[0:1, bass.ds(2 * i + h, 1)], min_val=0, max_val=NB - 1)
                    dve.wait_ge(summed, 2 * i + h + 1)
                    dve.wait_ge(added, 2 * i + h + 2)
                    into = total[:, bass.ds(at, 1), :].rearrange("p a d -> p (a d)")
                    if count is not None:
                        nc.vector.tensor_tensor(count[:, bass.ds(at, 1)], count[:, bass.ds(at, 1)],
                                                cnt_ps[h][0:BN, 0:1], ALU.add)
                    nc.vector.tensor_tensor(into, into, sum_ps[h][0:BN, :], ALU.add).then_inc(added, 1)


def row_on_all(row, partitions):
    return row.rearrange("(a n) -> a n", a=1).broadcast_to([partitions, row.shape[0]])


def weight_rows(w):
    return w.rearrange("(f p) n -> p f n", p=P)


def node_stage(pg, tag, loads, products, finish, scalar_finish=None):
    nc = pg.nc
    with ExitStack() as ctx:
        ps = [ctx.enter_context(nc.psum_tensor(f"{tag}_ps{i}", [P, D], FP32)) for i in range(2)]
        loaded, made, taken, chain, half, given = (ctx.enter_context(nc.semaphore(f"{tag}_{n}"))
                                                   for n in ("loaded", "made", "taken", "chain", "half", "given"))
        block = ctx.enter_context(nc.Block())

        @block.sync
        def _(sp):
            for to, src in loads:
                sp.dma_start(to, src).then_inc(loaded, 16)
            sp.wait_ge(loaded, 16 * len(loads))

        @block.tensor
        def _(pe):
            pe.wait_ge(loaded, 16 * len(loads))
            for b in range(NB):
                if b >= 2:
                    pe.wait_ge(taken, b - 1)
                products(b, ps[b % 2]).then_inc(made, 1)

        @block.vector
        def _(dve):
            done = [0]

            def link(ins):
                done[0] += 1
                ins.then_inc(chain, 1)
                dve.wait_ge(chain, done[0])

            dve.wait_ge(loaded, 16 * len(loads))
            for b in range(NB):
                dve.wait_ge(made, b + 1)
                finish(b, ps[b % 2][0:BN, :], link).then_inc(taken, 1)


def accumulate(nc, out, pairs):
    for n, (lhsT, rhs) in enumerate(pairs):
        last = nc.tensor.matmul(out, lhsT, rhs, start=(n == 0), stop=(n == len(pairs) - 1))
    return last


def nodes_of(b):
    return slice(b * BN, (b + 1) * BN)


def layer0(pg):
    nc = pg.nc
    pg.h_table = nc.dram_tensor("h_table", [NODES, D], FP32).ap()
    normalize(pg, "n0", pg.h_table)
    with ExitStack() as ctx:
        total = pg.sb("total0", [BN, NB, D], ctx=ctx)
        count = pg.sb("count0", [BN, NB], ctx=ctx)
        totalT = pg.sb("total0T", [P, 4, NODES], ctx=ctx)
        w = pg.sb("w0", [P, 8, D], ctx=ctx)
        bias = pg.sb("bias0", [BN, D], ctx=ctx)
        segment_sum(pg, "g0", pg.h_table, pg.src_row, total, count=count)
        with nc.semaphore("mean_chain") as chain, nc.Block() as block:
            @block.vector
            def _(dve):
                nc.vector.tensor_scalar(count[:, :], count[:, :], 1.0, None, ALU.max).then_inc(chain, 1)
                dve.wait_ge(chain, 1)
                nc.vector.reciprocal(count[:, :], count[:, :]).then_inc(chain, 1)
                dve.wait_ge(chain, 2)
                for b in range(NB):
                    nc.vector.tensor_scalar(total[:, b, :], total[:, b, :], count[:, b:b + 1], None, ALU.mult)
        transpose_nodes(pg, "t0", total, totalT, 4)

        def products(b, ps):
            return accumulate(nc, ps[0:BN, :], [(pg.hT[:, f, nodes_of(b)], w[:, f, :]) for f in range(4)]
                              + [(totalT[:, f, nodes_of(b)], w[:, 4 + f, :]) for f in range(4)])

        def finish(b, ps, link):
            link(nc.vector.tensor_tensor(pg.x[:, b, :], pg.x[:, b, :], ps, ALU.add))
            return nc.vector.tensor_tensor(pg.x[:, b, :], pg.x[:, b, :], bias[:, :], ALU.add)

        node_stage(pg, "w0s", [(w[:, :, :], weight_rows(pg.inp["L0_gnn_W"])),
                               (bias[:, :], row_on_all(pg.inp["L0_gnn_b"], BN))], products, finish)


def relation_tables(pg, tag, basis_in, comp_in, table):
    nc = pg.nc
    with ExitStack() as ctx:
        basis = pg.sb(f"{tag}_basis", [P, BASES, 4 * D], ctx=ctx)
        comp = pg.sb(f"{tag}_comp", [P, RELS * BASES], ctx=ctx)
        w = pg.sb(f"{tag}_w", [P, 2, 4 * D], ctx=ctx)
        rows = pg.sb(f"{tag}_rows", [BN, 2, NB, D], ctx=ctx)
        ps = [ctx.enter_context(nc.psum_tensor(f"{tag}_ps{i}", [P, D], FP32)) for i in range(2)]
        loaded, mixed, chain, used, made, taken = (ctx.enter_context(nc.semaphore(f"{tag}_{n}")) for n in
                                                   ("loaded", "mixed", "chain", "used", "made", "taken"))
        stored = [ctx.enter_context(nc.semaphore(f"{tag}_stored{i}")) for i in range(2)]
        block = ctx.enter_context(nc.Block())

        @block.sync
        def _(sp):
            sp.dma_start(comp[:, :], row_on_all(comp_in.rearrange("r b -> (r b)"), P)).then_inc(loaded, 16)
            for k in range(BASES):
                sp.dma_start(basis[:, k, :].rearrange("p (f n) -> p f n", f=4),
                             weight_rows(basis_in[k, :, :])).then_inc(loaded, 16)
            for r in range(RELS):
                sp.wait_ge(taken, NB * (r + 1))
                sp.dma_start(table[r * NODES:(r + 1) * NODES, :].rearrange("(b p) d -> p b d", p=BN),
                             rows[:, r % 2, :, :]).then_inc(stored[r % 2], 16)
            for n in range(2):
                sp.wait_ge(stored[n], 16 * RELS // 2)

        @block.vector
        def _(dve):
            dve.wait_ge(loaded, 16 * (BASES + 1))
            for r in range(RELS):
                if r >= 2:
                    dve.wait_ge(used, r - 1)
                for k in range(BASES):
                    c = comp[:, r * BASES + k:r * BASES + k + 1]
                    if k == 0:
                        ins = nc.vector.tensor_scalar(w[:, r % 2, :], basis[:, k, :], c, None, ALU.mult)
                    else:
                        ins = nc.vector.scalar_tensor_tensor(out=w[:, r % 2, :], in0=basis[:, k, :], scalar=c,
                                                             in1=w[:, r % 2, :], op0=ALU.mult, op1=ALU.add)
                    ins.then_inc(chain, 1)
                    dve.wait_ge(chain, BASES * r + k + 1)
                dve.sem_inc(mixed, 1)

        @block.tensor
        def _(pe):
            for r in range(RELS):
                pe.wait_ge(mixed, r + 1)
                for b in range(NB):
                    n = r * NB + b
                    if n >= 2:
                        pe.wait_ge(taken, n - 1)
                    accumulate(nc, ps[n % 2][0:BN, :],
                               [(pg.hT[:, f, nodes_of(b)], w[:, r % 2, f * D:(f + 1) * D])
                                for f in range(4)]).then_inc(made, 1)
                pe.wait_ge(made, (r + 1) * NB)
                pe.sem_inc(used, 1)

        @block.scalar
        def _(act):
            for r in range(RELS):
                if r >= 2:
                    act.wait_ge(stored[r % 2], 16 * (r // 2))
                for b in range(NB):
                    act.wait_ge(made, r * NB + b + 1)
                    nc.scalar.copy(rows[:, r % 2, b, :], ps[(r * NB + b) % 2][0:BN, :]).then_inc(taken, 1)


def layer1(pg):
    nc = pg.nc
    rel_table = nc.dram_tensor("rel_table", [RELS * NODES, D], FP32).ap()
    normalize(pg, "n1")
    for c in range(2):
        relation_tables(pg, f"rt{c}", pg.inp[f"L1_gnn_basis{c}"], pg.inp[f"L1_gnn_comp{c}"], rel_table)
        with ExitStack() as ctx:
            total = pg.sb(f"total1{c}", [BN, NB, D], ctx=ctx)
            loop_w = pg.sb(f"loop{c}", [P, 4, D], ctx=ctx)
            bias = pg.sb(f"bias1{c}", [BN, D], ctx=ctx)
            segment_sum(pg, f"g1{c}", rel_table, pg.rel_row, total,
                        weight=lambda t: pg.record[:, bass.ds(t, 1), WEIGHT])

            def products(b, ps):
                return accumulate(nc, ps[0:BN, :], [(pg.hT[:, f, nodes_of(b)], loop_w[:, f, :]) for f in range(4)])

            def finish(b, ps, link):
                link(nc.vector.tensor_tensor(total[:, b, :], total[:, b, :], ps, ALU.add))
                link(nc.vector.tensor_tensor(total[:, b, :], total[:, b, :], bias[:, :], ALU.add))
                if c == 0:
                    return nc.vector.tensor_scalar(pg.h[:, b, :], total[:, b, :], 0.0, None, ALU.max)
                return nc.vector.tensor_tensor(pg.x[:, b, :], pg.x[:, b, :], total[:, b, :], ALU.add)

            node_stage(pg, f"lw{c}", [(loop_w[:, :, :], weight_rows(pg.inp[f"L1_gnn_loop{c}"])),
                                      (bias[:, :], row_on_all(pg.inp[f"L1_gnn_bias{c}"], BN))], products, finish)
        if c == 0:
            transpose_nodes(pg, "t1", pg.h, pg.hT, 4)


def two_at_a_time(eng, body):
    with eng.Fori(0, NG // 2 - 1) as i:
        for h in range(2):
            body(2 * i + h, h, 0)
    body(NG - 2, 0, 1)
    body(NG - 1, 1, 2)


def hot_tiles(pg, dve, hot, hot_free, hot_ready, g, h):
    for k in range(TG):
        t = g * TG + k
        dve.wait_ge(hot_free, t + 1)
        pg.nc.vector.tensor_scalar(hot[:, h * TG + k, :], pg.iota_free[:, 0:BN],
                                   pg.dst_in_block[:, bass.ds(t, 1)], None, ALU.is_equal).then_inc(hot_ready, 1)


def message_pass(pg, tag, tableU, total):
    nc = pg.nc
    M = 8 * MUL
    with ExitStack() as ctx:
        got = pg.sb("u_got", [P, 2 * TG, D], ctx=ctx)
        idx = pg.sb("u_idx", [P, 2, TG], U32, ctx)
        hot = pg.sb("u_hot", [P, 2 * TG, BN], ctx=ctx)
        w1 = pg.sb("u_w1", [8, HID], ctx=ctx)
        w2 = pg.sb("u_w2", [HID, HID], ctx=ctx)
        w3 = pg.sb("u_w3", [HID, HID], ctx=ctx)
        w4 = pg.sb("u_w4", [HID, D], ctx=ctx)
        attrT = pg.sb("u_attrT", [8, 2, SG], ctx=ctx)
        hid = [pg.sb(f"u_hid{n}", [HID, SG], ctx=ctx) for n in range(2)]
        hid3 = pg.sb("u_hid3", [HID, 2, SG], ctx=ctx)
        t2 = pg.sb("u_t2", [P, 2, MUL], ctx=ctx)
        q = pg.sb("u_q", [P, 2, MUL], ctx=ctx)
        msg = pg.sb("u_msg", [P, 2, M], ctx=ctx)
        mlp_ps = ctx.enter_context(nc.psum_tensor("u_mlp_ps", [P, SG], FP32))
        tp_ps = [ctx.enter_context(nc.psum_tensor(f"u_tp_ps{n}", [P, D], FP32)) for n in range(2)]
        sum_ps = [ctx.enter_context(nc.psum_tensor(f"u_sum_ps{n}", [P, M], FP32)) for n in range(2)]
        sems = gather_sems(pg, ctx, "u")
        (loaded, cleared, hot_ready, hot_free, attr_free, layer_made, layer_done, tp_ready, t2_ready,
         q_chain, msg_dve, msg_act, summed, added, passed) = (ctx.enter_context(nc.semaphore(f"u_{n}")) for n in (
             "loaded", "cleared", "hot_ready", "hot_free", "attr_free", "layer_made", "layer_done",
             "tp_ready", "t2_ready", "q_chain", "msg_dve", "msg_act", "summed", "added", "pe_passed"))
        attr_in = [ctx.enter_context(nc.semaphore(f"u_attr_in{h}")) for h in range(2)]
        block = ctx.enter_context(nc.Block())

        @block.sync
        def _(sp):
            for to, src in ((w1, "W_mlp1"), (w2, "W_mlp2"), (w3, "W_mlp3"), (w4, "W_mlp4")):
                sp.dma_start(to[:, :], pg.inp[f"L2_gnn_{src}"]).then_inc(loaded, 16)
            sp.sem_inc(attr_free, 2)
            with sp.Fori(0, NG // 2) as i:
                for h in range(2):
                    sp.wait_ge(attr_free, 2 * i + h + 1)
                    sp.dma_start(attrT[:, h, :], pg.attrT[bass.ds(2 * i + h, 1), A8:SMALL, :]
                                 .rearrange("a r e -> (a r) e")).then_inc(attr_in[h], 16)

        @block.gpsimd
        def _(pool):
            nc.gpsimd.memset(total[:, :, :], 0.0).then_inc(cleared, 1)
            gather_loop(pg, pool, sems, tableU, pg.src_row, got, idx, D)

        @block.tensor
        def _(pe):
            def layer(g, h, n):
                if n == 0:
                    pe.wait_ge(attr_in[h], (g - h) * 8 + 16)
                else:
                    pe.wait_ge(layer_done, 3 * g + n)
                    pe.sem_inc(passed, 1)
                lhsT, rhs = ((w1, attrT[:, h, :]), (w2, hid[0][:, :]), (w3, hid[1][:, :]))[n]
                nc.tensor.matmul(mlp_ps[0:HID, :], lhsT[:, :], rhs, start=True, stop=True).then_inc(layer_made, 1)
                if n == 0:
                    pe.wait_ge(layer_made, 3 * g + 1)
                    pe.sem_inc(attr_free, 1)

            def path_weights(g, h, k):
                nc.tensor.matmul(tp_ps[k % 2][:, :], hid3[:, h, k * P:(k + 1) * P], w4[:, :],
                                 start=True, stop=True).then_inc(tp_ready, 1)

            def scatter(g, h, k):
                t = g * TG + k
                pe.wait_ge(msg_dve, t + 1)
                pe.wait_ge(msg_act, t + 2)
                if k == 0:
                    pe.wait_ge(added, g + 1)
                nc.tensor.matmul(sum_ps[h][0:BN, 0:D], hot[:, h * TG + k, :], msg[:, k % 2, 0:D],
                                 start=(k == 0), stop=(k == TG - 1))
                nc.tensor.matmul(sum_ps[h][0:BN, D:M], hot[:, h * TG + k, :], msg[:, k % 2, D:M],
                                 start=(k == 0), stop=(k == TG - 1)).then_inc(hot_free, 1)

            def body(g, h, last):
                more = last < 2
                pe.wait_ge(layer_done, 3 * g + 3)
                path_weights(g, h, 0)
                if more:
                    layer(g + 1, 1 - h, 0)
                path_weights(g, h, 1)
                scatter(g, h, 0)
                if more:
                    layer(g + 1, 1 - h, 1)
                path_weights(g, h, 2)
                scatter(g, h, 1)
                if more:
                    layer(g + 1, 1 - h, 2)
                path_weights(g, h, 3)
                scatter(g, h, 2)
                scatter(g, h, 3)
                pe.wait_ge(hot_free, (g + 1) * TG + 2 * TG)
                pe.sem_inc(summed, 1)

            pe.sem_inc(hot_free, 2 * TG)
            pe.wait_ge(loaded, 64)
            for n in range(3):
                layer(0, 0, n)
            pe.wait_ge(hot_ready, 2 * TG)
            two_at_a_time(pe, body)

        @block.scalar
        def _(act):
            def layer(g, h, n):
                act.wait_ge(layer_made, 3 * g + n + 1)
                scale = 1.0 / np.sqrt(8.0) if n == 0 else SILU_2MOM / np.sqrt(float(HID))
                to = (hid[0][:, :], hid[1][:, :], hid3[:, h, :])[n]
                nc.scalar.activation(to, mlp_ps[0:HID, :], ACT.Silu, scale=float(scale)).then_inc(layer_done, 1)

            def vector_paths(g, h, k):
                t = g * TG + k
                act.wait_ge(t2_ready, t + 1)
                for m in range(3):
                    last = nc.scalar.activation(msg[:, k % 2, (2 + m) * MUL:(3 + m) * MUL], t2[:, k % 2, :], ACT.Copy,
                                                scale=pg.record[:, bass.ds(t, 1), Y + 1 + m])
                last.then_inc(msg_act, 1)

            def body(g, h, last):
                more = last < 2
                if more:
                    layer(g + 1, 1 - h, 0)
                vector_paths(g, h, 0)
                if more:
                    layer(g + 1, 1 - h, 1)
                vector_paths(g, h, 1)
                if more:
                    layer(g + 1, 1 - h, 2)
                vector_paths(g, h, 2)
                vector_paths(g, h, 3)

            act.sem_inc(msg_act, 1)
            for n in range(3):
                layer(0, 0, n)
            two_at_a_time(act, body)

        @block.vector
        def _(dve):
            def paths(g, h, k):
                t = g * TG + k
                b = h * TG + k
                y = [pg.record[:, bass.ds(t, 1), Y + m] for m in range(4)]
                tp = tp_ps[k % 2]
                s0, s1 = got[:, b, 0:MUL], [got[:, b, (1 + m) * MUL:(2 + m) * MUL] for m in range(3)]
                dve.wait_ge(sems["arrived"][b], sems["before"] + (g - h) * 8 + 16)
                if k >= 2:
                    dve.wait_ge(hot_free, g * TG + k - 1 + 2 * TG)
                else:
                    dve.wait_ge(hot_free, g * TG + k - 1 + 2 * TG)
                nc.vector.tensor_scalar(q[:, k % 2, :], s1[0], y[1], None, ALU.mult).then_inc(q_chain, 1)
                dve.wait_ge(tp_ready, t + 1)
                dve.wait_ge(msg_act, t)
                nc.vector.tensor_tensor(t2[:, k % 2, :], tp[:, MUL:2 * MUL], s0, ALU.mult).then_inc(t2_ready, 1)
                nc.vector.scalar_tensor_tensor(out=msg[:, k % 2, 0:MUL], in0=tp[:, 0:MUL], scalar=y[0], in1=s0,
                                               op0=ALU.mult, op1=ALU.mult)
                dve.wait_ge(q_chain, 3 * t + 1)
                nc.vector.scalar_tensor_tensor(out=q[:, k % 2, :], in0=s1[1], scalar=y[2], in1=q[:, k % 2, :],
                                               op0=ALU.mult, op1=ALU.add).then_inc(q_chain, 1)
                nc.vector.scalar_tensor_tensor(
                    out=msg[:, k % 2, 5 * MUL:8 * MUL].rearrange("p (m u) -> p m u", m=3),
                    in0=tp[:, 2 * MUL:3 * MUL].rearrange("p (a u) -> p a u", a=1).broadcast_to([P, 3, MUL]),
                    scalar=y[0], in1=got[:, b, MUL:D].rearrange("p (m u) -> p m u", m=3),
                    op0=ALU.mult, op1=ALU.mult)
                dve.wait_ge(q_chain, 3 * t + 2)
                nc.vector.scalar_tensor_tensor(out=q[:, k % 2, :], in0=s1[2], scalar=y[3], in1=q[:, k % 2, :],
                                               op0=ALU.mult, op1=ALU.add).then_inc(q_chain, 1)
                dve.wait_ge(q_chain, 3 * t + 3)
                nc.vector.tensor_tensor(msg[:, k % 2, MUL:2 * MUL], tp[:, 3 * MUL:4 * MUL], q[:, k % 2, :],
                                        ALU.mult).then_inc(msg_dve, 1)
                if k == TG - 1:
                    dve.wait_ge(msg_dve, t + 1)
                    dve.sem_inc(sems["gather_free"], TG)

            def body(g, h, last):
                for k in range(TG):
                    paths(g, h, k)
                at = nc.vector.value_load(pg.block_of_group[0:1, bass.ds(g, 1)], min_val=0, max_val=NB - 1)
                dve.wait_ge(summed, g + 1)
                dve.wait_ge(added, g + 2)
                into = total[:, bass.ds(at, 1), :].rearrange("p a d -> p (a d)")
                nc.vector.tensor_tensor(into, into, sum_ps[h][0:BN, :], ALU.add).then_inc(added, 1)
                if last == 0:
                    hot_tiles(pg, dve, hot, hot_free, hot_ready, g + 2, h)

            dve.sem_inc(sems["gather_free"], 2 * TG)
            dve.sem_inc(added, 2)
            hot_tiles(pg, dve, hot, hot_free, hot_ready, 0, 0)
            hot_tiles(pg, dve, hot, hot_free, hot_ready, 1, 1)
            dve.wait_ge(cleared, 1)
            two_at_a_time(dve, body)


def layer2(pg):
    nc = pg.nc
    normalize(pg, "n2")
    tableU = nc.dram_tensor("up_table", [NODES, D], FP32).ap()
    with ExitStack() as ctx:
        total = pg.sb("total2", [BN, NB, 8 * MUL], ctx=ctx)
        with ExitStack() as up:
            split = pg.sb("split", [BN, NB, D], ctx=up)
            splitT = pg.sb("splitT", [P, 4, NODES], ctx=up)
            w_up = pg.sb("w_up", [P, 2, MUL], ctx=up)
            rows = pg.sb("up_rows", [BN, NB, D], ctx=up)
            with nc.Block() as block:
                @block.vector
                def _(dve):
                    nc.vector.tensor_copy(split[:, :, 0:MUL], pg.h[:, :, 0:MUL])
                    for b in range(NB):
                        nc.vector.tensor_copy(split[:, b, MUL:D].rearrange("p (m u) -> p m u", m=3),
                                              pg.h[:, b, MUL:D].rearrange("p (u m) -> p m u", m=3))
            transpose_nodes(pg, "t2", split, splitT, 4)

            def products(b, ps):
                for f in range(4):
                    last = nc.tensor.matmul(ps[0:BN, f * MUL:(f + 1) * MUL], splitT[:, f, nodes_of(b)],
                                            w_up[:, min(f, 1), :], start=True, stop=True)
                return last

            node_stage(pg, "up", [(w_up[:, 0, :], pg.inp["L2_gnn_W_up0"]), (w_up[:, 1, :], pg.inp["L2_gnn_W_up1"])],
                       products, lambda b, ps, link: nc.vector.tensor_copy(rows[:, b, :], ps))
            with nc.semaphore("up_out") as stored, nc.Block() as block:
                @block.sync
                def _(sp):
                    sp.dma_start(tableU.rearrange("(b p) d -> p b d", p=BN), rows[:, :, :]).then_inc(stored, 16)
                    sp.wait_ge(stored, 16)
        message_pass(pg, "u", tableU, total)
        totalT = pg.sb("total2T", [P, 8, NODES], ctx=ctx)
        w_out = pg.sb("w_out", [P, 4, MUL], ctx=ctx)
        transpose_nodes(pg, "t3", total, totalT, 8)
        with nc.Block() as block:
            pass
        scale = SILU_2MOM / np.sqrt(float(HID)) / np.sqrt(float(MUL)) / np.sqrt(2.0 * MUL) / 10.0
        tmp = pg.sb("out_tmp", [BN, MUL], ctx=ctx)

        def products(b, ps):
            outs = [((0,), (0,)), ((2, 5), (2, 3)), ((3, 6), (2, 3)), ((4, 7), (2, 3))]
            for n, (blocks, ws) in enumerate(outs):
                accumulate(nc, ps[0:BN, n * MUL:(n + 1) * MUL],
                           [(totalT[:, f, nodes_of(b)], w_out[:, w, :]) for f, w in zip(blocks, ws)])
            return nc.tensor.matmul(p4_ps[b % 2][0:BN, 0:MUL], totalT[:, 1, nodes_of(b)], w_out[:, 1, :],
                                    start=True, stop=True)

        def finish(b, ps, link):
            link(nc.vector.scalar_tensor_tensor(out=pg.x[:, b, 0:MUL], in0=ps[:, 0:MUL], scalar=float(scale),
                                                in1=pg.x[:, b, 0:MUL], op0=ALU.mult, op1=ALU.add))
            link(nc.vector.scalar_tensor_tensor(out=pg.x[:, b, 0:MUL], in0=p4_ps[b % 2][0:BN, 0:MUL],
                                                scalar=float(scale / np.sqrt(3.0)), in1=pg.x[:, b, 0:MUL],
                                                op0=ALU.mult, op1=ALU.add))
            xv = pg.x[:, b, MUL:D].rearrange("p (u m) -> p m u", m=3)
            return nc.vector.scalar_tensor_tensor(out=xv, in0=ps[:, MUL:D].rearrange("p (m u) -> p m u", m=3),
                                                  scalar=float(scale), in1=xv, op0=ALU.mult, op1=ALU.add)

        with ExitStack() as banks:
            p4_ps = [banks.enter_context(nc.psum_tensor(f"p4_ps{n}", [P, D], FP32)) for n in range(2)]
            node_stage(pg, "out", [(w_out[:, 0:2, :], weight_rows(pg.inp["L2_gnn_W_out0"])),
                                   (w_out[:, 2:4, :], weight_rows(pg.inp["L2_gnn_W_out1"]))], products, finish)


def edge_mlp_pass(pg, table_src, by_dst, w_attr, w2, bias2, total):
    nc = pg.nc
    with ExitStack() as ctx:
        got = pg.sb("e_got", [P, 2 * TG, D], ctx=ctx)
        idx = pg.sb("e_idx", [P, 2, TG], U32, ctx)
        hot = pg.sb("e_hot", [P, 2 * TG, BN], ctx=ctx)
        hotT = pg.sb("e_hotT", [BN, SG], ctx=ctx)
        dst_part = pg.sb("e_dst_part", [BN, D], ctx=ctx)
        attrT = pg.sb("e_attrT", [HID, 2, SG], ctx=ctx)
        first = pg.sb("e_first", [P, 2, 4, SG], ctx=ctx)
        msg = pg.sb("e_msg", [P, 2, D], ctx=ctx)
        act1 = pg.sb("e_act1", [P, 2, SG], ctx=ctx)
        act2 = pg.sb("e_act2", [P, 2, SG], ctx=ctx)
        lin2 = pg.sb("e_lin2", [P, 2, SG], ctx=ctx)
        hotT_ps = ctx.enter_context(nc.psum_tensor("e_hotT_ps", [P, SG], FP32))
        pre_ps = [ctx.enter_context(nc.psum_tensor(f"e_pre_ps{n}", [P, SG], FP32)) for n in range(2)]
        two_ps = [ctx.enter_context(nc.psum_tensor(f"e_two_ps{n}", [P, SG], FP32)) for n in range(2)]
        sum_ps = [ctx.enter_context(nc.psum_tensor(f"e_sum_ps{n}", [P, D], FP32)) for n in range(2)]
        sems = gather_sems(pg, ctx, "e")
        (cleared, hot_ready, hot_free, attr_free, hotT_turned, group_ready, pre_ready, act1_chain, act2_chain,
         den1_ready, den2_ready, rec1_chain, rec2_chain, first_done, two_biased, two_ready, msg_done, summed, added) = (
            ctx.enter_context(nc.semaphore(f"e_{n}")) for n in (
                "cleared", "hot_ready", "hot_free", "attr_free", "hotT_turned", "group_ready", "pre_ready",
                "act1_chain", "act2_chain", "den1_ready", "den2_ready", "rec1_chain", "rec2_chain", "first_done",
                "two_biased",
                "two_ready", "msg_done", "summed", "added"))
        attr_in = [ctx.enter_context(nc.semaphore(f"e_attr_in{h}")) for h in range(2)]
        block = ctx.enter_context(nc.Block())

        @block.sync
        def _(sp):
            sp.sem_inc(attr_free, 2)
            with sp.Fori(0, NG // 2) as i:
                for h in range(2):
                    sp.wait_ge(attr_free, 2 * i + h + 1)
                    sp.dma_start(attrT[:, h, :], pg.attrT[bass.ds(2 * i + h, 1), A64:A8, :]
                                 .rearrange("a r e -> (a r) e")).then_inc(attr_in[h], 16)

        @block.gpsimd
        def _(pool):
            nc.gpsimd.memset(total[:, :, :], 0.0).then_inc(cleared, 1)
            gather_loop(pg, pool, sems, table_src, pg.src_row, got, idx, D)

        @block.tensor
        def _(pe):
            def turn_hot(g, h):
                pe.wait_ge(hot_ready, (g + 1) * TG)
                for k in range(TG):
                    last = nc.tensor.transpose(hotT_ps[0:BN, k * P:(k + 1) * P], hot[:, h * TG + k, :], pg.ident[:, :])
                last.then_inc(hotT_turned, 1)

            def first_layer(g, h, f):
                cols = slice(f * P, (f + 1) * P)
                pe.wait_ge(first_done, 4 * g + f + 1)
                if f == 0:
                    pe.wait_ge(group_ready, 2 * g + 2)
                    pe.wait_ge(attr_in[h], (g - h) * 8 + 16)
                    for k in range(TG):
                        pe.wait_ge(sems["arrived"][h * TG + k], sems["before"] + (g - h) * 8 + 16)
                nc.tensor.matmul(pre_ps[f % 2][:, :], dst_part[:, cols], hotT[:, :], start=True, stop=False)
                nc.tensor.matmul(pre_ps[f % 2][:, :], w_attr[:, cols], attrT[:, h, :], start=False, stop=False)
                for k in range(TG):
                    last = nc.tensor.matmul(pre_ps[f % 2][:, k * P:(k + 1) * P], got[:, h * TG + k, cols],
                                            pg.ident[:, :], start=False, stop=(k == TG - 1))
                last.then_inc(pre_ready, 1)
                if f == 3:
                    pe.wait_ge(pre_ready, 4 * g + 4)
                    pe.sem_inc(attr_free, 1)
                    pe.sem_inc(sems["gather_free"], TG)

            def second_layer(g, h, k):
                pe.wait_ge(first_done, 4 * g + 4 + 2)
                pe.wait_ge(two_biased, 4 * g + k + 1)
                accumulate(nc, two_ps[k % 2][:, :],
                           [(first[:, h, f, k * P:(k + 1) * P], w2[:, f, :]) for f in range(4)]).then_inc(two_ready, 1)

            def scatter(g, h, k):
                pe.wait_ge(msg_done, 4 * g + k + 3)
                if k == 0:
                    pe.wait_ge(added, g + 1)
                nc.tensor.matmul(sum_ps[h][0:BN, :], hot[:, h * TG + k, :], msg[:, k % 2, :],
                                 start=(k == 0), stop=(k == TG - 1)).then_inc(hot_free, 1)

            def body(g, h, last):
                more = last < 2
                if more:
                    turn_hot(g + 1, 1 - h)
                second_layer(g, h, 0)
                if more:
                    first_layer(g + 1, 1 - h, 0)
                second_layer(g, h, 1)
                if more:
                    first_layer(g + 1, 1 - h, 1)
                scatter(g, h, 0)
                second_layer(g, h, 2)
                if more:
                    first_layer(g + 1, 1 - h, 2)
                scatter(g, h, 1)
                second_layer(g, h, 3)
                if more:
                    first_layer(g + 1, 1 - h, 3)
                scatter(g, h, 2)
                scatter(g, h, 3)
                pe.wait_ge(hot_free, (g + 1) * TG + 2 * TG)
                pe.sem_inc(summed, 1)

            pe.sem_inc(hot_free, 2 * TG)
            turn_hot(0, 0)
            for f in range(4):
                first_layer(0, 0, f)
            two_at_a_time(pe, body)

        @block.scalar
        def _(act):
            def group_rows(g, h):
                at = nc.scalar.value_load(pg.block_of_group[0:1, bass.ds(g, 1)], min_val=0, max_val=NB - 1)
                act.wait_ge(hotT_turned, g + 1)
                nc.scalar.copy(hotT[:, :], hotT_ps[0:BN, :]).then_inc(group_ready, 1)
                nc.scalar.copy(dst_part[:, :], by_dst[:, bass.ds(at, 1), :].rearrange("p a d -> p (a d)"))\
                    .then_inc(group_ready, 1)

            def half_mish(n, done, chain, den_ready, buf, x):
                act.wait_ge(done, n + 1)
                nc.scalar.activation(buf, x, ACT.Exp).then_inc(chain, 1)
                act.wait_ge(chain, 2 * n + 1)
                nc.scalar.activation(buf, buf, ACT.Square, bias=pg.ones[:, 0:1]).then_inc(chain, 1)
                act.wait_ge(chain, 2 * n + 2)
                nc.scalar.activation(buf, buf, ACT.Identity, scale=-0.5,
                                     bias=pg.minus_half[:, 0:1]).then_inc(den_ready, 1)

            def one(g, f):
                act.wait_ge(pre_ready, 4 * g + f + 1)
                half_mish(4 * g + f, first_done, act1_chain, den1_ready, act1[:, f % 2, :], pre_ps[f % 2][:, :])

            def two(g, k):
                act.wait_ge(two_biased, 4 * g + k + 3)
                half_mish(4 * g + k, msg_done, act2_chain, den2_ready, act2[:, k % 2, :], lin2[:, k % 2, :])

            group_rows(0, 0)
            for f in range(4):
                one(0, f)

            def body(g, h, last):
                more = last < 2
                if more:
                    group_rows(g + 1, 1 - h)
                for k in range(4):
                    two(g, k)
                    if more:
                        one(g + 1, k)

            two_at_a_time(act, body)

        @block.vector
        def _(dve):
            def one(g, h, f):
                n = 4 * g + f
                dve.wait_ge(den1_ready, n + 1)
                nc.vector.reciprocal(act1[:, f % 2, :], act1[:, f % 2, :]).then_inc(rec1_chain, 1)
                dve.wait_ge(rec1_chain, n + 1)
                nc.vector.scalar_tensor_tensor(out=first[:, h, f, :], in0=act1[:, f % 2, :], scalar=1.0,
                                               in1=pre_ps[f % 2][:, :], op0=ALU.add, op1=ALU.mult)\
                    .then_inc(first_done, 1)

            def add_bias(g, k):
                dve.wait_ge(two_ready, 4 * g + k + 1)
                nc.vector.tensor_tensor(lin2[:, k % 2, :], two_ps[k % 2][:, :], bias2[:, :], ALU.add)\
                    .then_inc(two_biased, 1)

            def two(g, k):
                n = 4 * g + k
                dve.wait_ge(den2_ready, n + 1)
                nc.vector.reciprocal(act2[:, k % 2, :], act2[:, k % 2, :]).then_inc(rec2_chain, 1)
                dve.wait_ge(rec2_chain, n + 1)
                dve.wait_ge(hot_free, n - 1 + 2 * TG)
                nc.vector.scalar_tensor_tensor(out=msg[:, k % 2, :], in0=act2[:, k % 2, :], scalar=1.0,
                                               in1=lin2[:, k % 2, :], op0=ALU.add, op1=ALU.mult)\
                    .then_inc(msg_done, 1)

            def body(g, h, last):
                more = last < 2
                add_bias(g, 0)
                for k in range(4):
                    two(g, k)
                    if more:
                        one(g + 1, 1 - h, k)
                    if k < 3:
                        add_bias(g, k + 1)
                at = nc.vector.value_load(pg.block_of_group[0:1, bass.ds(g, 1)], min_val=0, max_val=NB - 1)
                dve.wait_ge(summed, g + 1)
                dve.wait_ge(added, g + 2)
                into = total[:, bass.ds(at, 1), :].rearrange("p a d -> p (a d)")
                nc.vector.tensor_tensor(into, into, sum_ps[h][0:BN, :], ALU.add).then_inc(added, 1)
                if last == 0:
                    hot_tiles(pg, dve, hot, hot_free, hot_ready, g + 2, h)

            dve.sem_inc(sems["gather_free"], 2 * TG)
            dve.sem_inc(added, 2)
            dve.sem_inc(first_done, 2)
            dve.sem_inc(two_biased, 2)
            dve.sem_inc(msg_done, 2)
            hot_tiles(pg, dve, hot, hot_free, hot_ready, 0, 0)
            hot_tiles(pg, dve, hot, hot_free, hot_ready, 1, 1)
            for f in range(4):
                one(0, 0, f)
            dve.wait_ge(cleared, 1)
            two_at_a_time(dve, body)


def layer3(pg):
    nc = pg.nc
    normalize(pg, "n3")
    table = nc.dram_tensor("src_table", [NODES, D], FP32).ap()
    w1 = pg.inp["L3_gnn_W1"]
    with ExitStack() as ctx:
        total = pg.sb("total3", [BN, NB, D], ctx=ctx)
        with ExitStack() as edges:
            by_dst = pg.sb("by_dst", [BN, NB, D], ctx=edges)
            w_attr = pg.sb("w_attr", [HID, D], ctx=edges)
            w2 = pg.sb("w2", [P, 4, D], ctx=edges)
            bias2 = pg.sb("bias2", [P, D], ctx=edges)
            with ExitStack() as early:
                w_src = pg.sb("w_src", [P, 4, D], ctx=early)
                w_dst = pg.sb("w_dst", [P, 4, D], ctx=early)
                bias1 = pg.sb("bias1", [BN, D], ctx=early)
                rows = pg.sb("src_rows", [BN, NB, D], ctx=early)
                node_stage(pg, "ws", [(w_src[:, :, :], weight_rows(w1[0:D, :])),
                                      (w_attr[:, :], w1[2 * D:2 * D + HID, :])],
                           lambda b, ps: accumulate(nc, ps[0:BN, :], [(pg.hT[:, f, nodes_of(b)], w_src[:, f, :])
                                                                      for f in range(4)]),
                           lambda b, ps, link: nc.vector.tensor_copy(rows[:, b, :], ps))
                with nc.semaphore("src_out") as stored, nc.Block() as block:
                    @block.sync
                    def _(sp):
                        sp.dma_start(table.rearrange("(b p) d -> p b d", p=BN), rows[:, :, :]).then_inc(stored, 16)
                        sp.wait_ge(stored, 16)
                node_stage(pg, "wd", [(w_dst[:, :, :], weight_rows(w1[D:2 * D, :])),
                                      (bias1[:, :], row_on_all(pg.inp["L3_gnn_b1"], BN)),
                                      (w2[:, :, :], weight_rows(pg.inp["L3_gnn_W2"])),
                                      (bias2[:, :], row_on_all(pg.inp["L3_gnn_b2"], P))],
                           lambda b, ps: accumulate(nc, ps[0:BN, :], [(pg.hT[:, f, nodes_of(b)], w_dst[:, f, :])
                                                                      for f in range(4)]),
                           lambda b, ps, link: nc.vector.tensor_tensor(by_dst[:, b, :], ps, bias1[:, :], ALU.add))
            edge_mlp_pass(pg, table, by_dst, w_attr, w2, bias2, total)
        totalT = pg.sb("total3T", [P, 4, NODES], ctx=ctx)
        transpose_nodes(pg, "t4", total, totalT, 4)
        w3 = pg.sb("w3", [P, 8, D], ctx=ctx)
        w4 = pg.sb("w4", [P, 4, D], ctx=ctx)
        rows = {n: pg.sb(f"{n}_row", [BN, D], ctx=ctx) for n in ("b3", "b4", "gamma", "beta")}
        u = pg.sb("u_nodes", [BN, NB, D], ctx=ctx)
        e = pg.sb("e_nodes", [BN, NB, D], ctx=ctx)
        node_stage(pg, "w3s", [(w3[:, :, :], weight_rows(pg.inp["L3_gnn_W3"])),
                               (rows["b3"][:, :], row_on_all(pg.inp["L3_gnn_b3"], BN))],
                   lambda b, ps: accumulate(nc, ps[0:BN, :],
                                            [(pg.hT[:, f, nodes_of(b)], w3[:, f, :]) for f in range(4)]
                                            + [(totalT[:, f, nodes_of(b)], w3[:, 4 + f, :]) for f in range(4)]),
                   lambda b, ps, link: nc.vector.tensor_tensor(u[:, b, :], ps, rows["b3"][:, :], ALU.add))
        with nc.semaphore("mish_act") as acts, nc.semaphore("mish_dve") as dves, nc.Block() as block:
            @block.scalar
            def _(act):
                nc.scalar.activation(e[:, :, :], u[:, :, :], ACT.Exp).then_inc(acts, 1)
                act.wait_ge(acts, 1)
                nc.scalar.activation(e[:, :, :], e[:, :, :], ACT.Square, bias=pg.ones[0:BN, 0:1]).then_inc(acts, 1)
                act.wait_ge(acts, 2)
                nc.scalar.activation(e[:, :, :], e[:, :, :], ACT.Identity, scale=-0.5,
                                     bias=pg.minus_half[0:BN, 0:1]).then_inc(acts, 1)

            @block.vector
            def _(dve):
                dve.wait_ge(acts, 3)
                nc.vector.reciprocal(e[:, :, :], e[:, :, :]).then_inc(dves, 1)
                dve.wait_ge(dves, 1)
                nc.vector.scalar_tensor_tensor(out=u[:, :, :], in0=e[:, :, :], scalar=1.0, in1=u[:, :, :],
                                               op0=ALU.add, op1=ALU.mult)
        transpose_nodes(pg, "t5", u, totalT, 4)

        def finish(b, ps, link):
            link(nc.vector.tensor_tensor(e[:, b, :], pg.h[:, b, :], ps, ALU.add))
            return nc.vector.tensor_tensor(e[:, b, :], e[:, b, :], rows["b4"][:, :], ALU.add)

        node_stage(pg, "w4s", [(w4[:, :, :], weight_rows(pg.inp["L3_gnn_W4"]))]
                   + [(rows[n][:, :], row_on_all(pg.inp[f"L3_gnn_{n}"], BN)) for n in ("b4", "gamma", "beta")],
                   lambda b, ps: accumulate(nc, ps[0:BN, :], [(totalT[:, f, nodes_of(b)], w4[:, f, :])
                                                              for f in range(4)]), finish)
        stats = pg.sb("f_stats", [BN, NB, 6], ctx=ctx)
        mv = pg.sb("f_mv", [BN, NB, 2], ctx=ctx)
        sd = pg.sb("f_sd", [BN, NB], ctx=ctx)
        rs = pg.sb("f_rs", [BN, NB], ctx=ctx)
        with ExitStack() as sems:
            chain, var, root, final, stored = (sems.enter_context(nc.semaphore(f"f_{n}"))
                                               for n in ("chain", "var", "root", "final", "stored"))
            block = sems.enter_context(nc.Block())

            @block.scalar
            def _(act):
                act.wait_ge(var, 1)
                nc.scalar.sqrt(sd[:, :], sd[:, :]).then_inc(root, 1)

            @block.vector
            def _(dve):
                done = [0]

                def link(ins):
                    done[0] += 1
                    ins.then_inc(chain, 1)
                    dve.wait_ge(chain, done[0])

                for b in range(NB):
                    last = nc.vector.bn_stats(out=stats[:, b, :], in_=e[:, b, :])
                link(last)
                for b in range(NB):
                    last = nc.vector.bn_aggr(out=mv[:, b, :], in_=stats[:, b, :])
                link(last)
                nc.vector.tensor_scalar(sd[:, :], mv[:, :, 1], EPS, None, ALU.add).then_inc(var, 1)
                dve.wait_ge(root, 1)
                link(nc.vector.reciprocal(rs[:, :], sd[:, :]))
                for b in range(NB):
                    link(nc.vector.tensor_scalar(e[:, b, :], e[:, b, :], mv[:, b, 0:1], rs[:, b:b + 1],
                                                 ALU.subtract, ALU.mult))
                    link(nc.vector.tensor_tensor(e[:, b, :], e[:, b, :], rows["gamma"][:, :], ALU.mult))
                    link(nc.vector.tensor_tensor(e[:, b, :], e[:, b, :], rows["beta"][:, :], ALU.add))
                    nc.vector.tensor_tensor(pg.x[:, b, :], pg.x[:, b, :], e[:, b, :], ALU.add).then_inc(final, 1)

            @block.sync
            def _(sp):
                for b in range(NB):
                    sp.wait_ge(final, b + 1)
                    sp.dma_start(pg.out[nodes_of(b), :], pg.x[:, b, :]).then_inc(stored, 16)
                sp.wait_ge(stored, 16 * NB)


STAGES = [constants, place_edges, order_edges, fetch_records, load_nodes, layer0, layer1, layer2, layer3]


OUT_SHAPE = (NODES, D)


def build(nc, args, out):
    pg = Program(nc, args, out)
    with pg.keep:
        for stage in STAGES:
            stage(pg)
            nc.all_engine_barrier(sems_to_clear=range(pg.arrived[-1].num + 1, max(nc.free_semaphores) + 1))


def kernel(**inputs):
    import concourse.bacc as bacc
    from concourse.bass_utils import run_bass_kernel_spmd

    data = {name: np.asarray(a) for name, a in inputs.items()}
    data["edge_floats"] = np.concatenate(
        [data.pop("edge_attr_64"), data.pop("edge_attr_8"), data.pop("edge_attr_4"),
         data.pop("edge_weight")[:, None], np.zeros((EDGES, RECORD - SRC), np.float32)], axis=1)
    data["L0_gnn_W"] = data["L0_gnn_W"].T

    nc = bacc.Bacc("TRN2", target_bir_lowering=False, num_devices=1)
    arrays, args = {}, {}
    for name, a in data.items():
        a = np.ascontiguousarray(a)
        arrays[f"in_{name}_dram"] = a
        args[name] = nc.dram_tensor(f"in_{name}_dram", a.shape, mybir.dt.from_np(a.dtype), kind="ExternalInput").ap()
    out = nc.dram_tensor("out_0_dram", OUT_SHAPE, FP32, kind="ExternalOutput").ap()
    build(nc, args, out)
    result = run_bass_kernel_spmd(nc, [arrays], core_ids=[0])
    return result.results[0]["out_0_dram"]
```

```python
import numpy as np
import concourse.bass as bass
from concourse import mybir
from contextlib import ExitStack

FP32 = mybir.dt.float32
BF16 = mybir.dt.bfloat16
I32 = mybir.dt.int32
U32 = mybir.dt.uint32
ALU = mybir.AluOpType
ACT = mybir.ActivationFunctionType

P = 128
NODES, D, EDGES = 625, 512, 20000
NB, BN = 5, 125
EP = 125
EC = EDGES // EP
TG = 4
SG = TG * P
RING = 4
NG = (EDGES + NB * (SG - 1)) // SG
NG += -NG % RING
NT = NG * TG
RECORD = 80
A64, A8, SMALL, SRC, DST, TYPE = 0, 64, 72, 77, 78, 79
Y, WEIGHT = 0, 4
RELS, BASES = 8, 4
MUL, HID = 128, 64
SILU_2MOM = 1.679177
EPS = 1e-5
LIMIT = 20.0


class Program:

    def __init__(self, nc, args, out):
        self.nc, self.inp, self.out = nc, args, out
        self.keep = ExitStack()

    def sb(self, name, shape, dt=FP32, ctx=None):
        return (ctx or self.keep).enter_context(self.nc.sbuf_tensor(name, shape, dt))


def constants(pg):
    nc = pg.nc
    pg.iota_free = pg.sb("iota_free", [P, NT])
    pg.ident = pg.sb("ident", [P, P])
    pg.ones = pg.sb("ones", [P, P])
    pg.ident16 = pg.sb("ident16", [P, P], BF16)
    pg.before = pg.sb("before", [P, P])
    pg.ln2 = pg.sb("ln2", [P, 1])
    pg.arrived = [pg.keep.enter_context(nc.semaphore(f"arrived{b}")) for b in range(RING * TG)]
    pg.landed = [0] * (RING * TG)
    with nc.semaphore("filled") as filled, nc.Block() as block:

        @block.gpsimd
        def _(pool):
            nc.gpsimd.iota(pg.iota_free[:, :], [[1, NT]], base=0, channel_multiplier=0,
                           allow_small_or_imprecise_dtypes=True)
            nc.gpsimd.memset(pg.ln2[:, :], float(np.log(2.0)))
            nc.gpsimd.memset(pg.ident[:, :], 0.0).then_inc(filled, 1)
            nc.gpsimd.memset(pg.ones[:, :], 1.0).then_inc(filled, 1)
            pool.wait_ge(filled, 2)
            nc.gpsimd.affine_select(out=pg.ident[:, :], in_=pg.ident[:, :], compare_op=ALU.not_equal, fill=1.0,
                                    base=0, pattern=[[-1, P]], channel_multiplier=1).then_inc(filled, 1)
            pool.wait_ge(filled, 3)
            nc.gpsimd.tensor_copy(pg.ident16[:, :], pg.ident[:, :])
            nc.gpsimd.affine_select(out=pg.before[:, :], in_=pg.ones[:, :], compare_op=ALU.is_gt, fill=0.0,
                                    base=0, pattern=[[1, P]], channel_multiplier=-1)


def place_edges(pg):
    nc = pg.nc
    ctx = ExitStack()
    pg.lane = pg.sb("lane", [EP, EC])
    pg.tile = pg.sb("tile", [EP, EC])
    pg.edge1 = pg.sb("edge1", [EP, EC])
    pg.block_of_tile = pg.sb("block_of_tile", [P, NT])
    pg.block_of_group = pg.sb("block_of_group", [1, NG], I32)
    pg.records = nc.dram_tensor("records", [EDGES, RECORD], FP32).ap()
    with ctx, ExitStack() as psums:
        dst_i = pg.sb("dst_i", [EP, EC], I32, ctx)
        dst = pg.sb("dst", [EP, EC], ctx=ctx)
        block_of = pg.sb("block_of", [EP, EC], ctx=ctx)
        over = pg.sb("over", [EP, EC], ctx=ctx)
        zero = pg.sb("zero", [EP, EC], ctx=ctx)
        mine = pg.sb("mine", [EP, NB, EC], ctx=ctx)
        rank = pg.sb("rank", [EP, NB, EC], ctx=ctx)
        in_row = pg.sb("in_row", [EP, NB], ctx=ctx)
        total = pg.sb("total", [P, NB], ctx=ctx)
        group_edge = pg.sb("group_edge", [P, 40], ctx=ctx)
        full = pg.sb("full", [P, 40], ctx=ctx)
        groups = pg.sb("groups", [P, NB], ctx=ctx)
        first_group = pg.sb("first_group", [P, NB + 1], ctx=ctx)
        shift = pg.sb("shift", [EP, NB], ctx=ctx)
        slot = pg.sb("slot", [EP, EC], ctx=ctx)
        slot_i = pg.sb("slot_i", [EP, EC], I32, ctx)
        lane_i = pg.sb("lane_i", [EP, EC], I32, ctx)
        tile_i = pg.sb("tile_i", [EP, EC], I32, ctx)
        group_no = pg.sb("group_no", [P, NG], ctx=ctx)
        group_blk = pg.sb("group_blk", [P, NG], ctx=ctx)
        record = pg.sb("record", [EP, EC, RECORD], ctx=ctx)
        ints = pg.sb("ints", [EP, 3, EC], I32, ctx)
        row_ps = psums.enter_context(nc.psum_tensor("row_ps", [P, 512], FP32))
        sem = {n: psums.enter_context(nc.semaphore(n)) for n in
               ("dst_in", "record_in", "ints_in", "iota_done", "chain", "rows_counted", "rows_summed",
                "record_built", "record_out")}
        block = psums.enter_context(nc.Block())

        @block.sync
        def _(sp):
            sp.dma_start(dst_i[:, :], pg.inp["dst"].rearrange("(p j) -> p j", j=EC)).then_inc(sem["dst_in"], 16)
            sp.dma_start(record[:, :, :].rearrange("p j r -> p (j r)"),
                         pg.inp["edge_floats"].rearrange("(p j) r -> p (j r)", j=EC)).then_inc(sem["record_in"], 16)
            for n, name in enumerate(("src", "dst", "edge_type_8")):
                sp.dma_start(ints[:, n, :], pg.inp[name].rearrange("(p j) -> p j", j=EC)).then_inc(sem["ints_in"], 16)
            sp.wait_ge(sem["record_built"], 3)
            sp.dma_start(pg.records.rearrange("(p j) r -> p (j r)", j=EC),
                         record[:, :, :].rearrange("p j r -> p (j r)")).then_inc(sem["record_out"], 16)
            sp.wait_ge(sem["record_out"], 16)

        @block.gpsimd
        def _(pool):
            nc.gpsimd.iota(group_edge[:, :], [[SG, 40]], base=0, channel_multiplier=0,
                           allow_small_or_imprecise_dtypes=True)
            nc.gpsimd.iota(group_no[:, :], [[1, NG]], base=0, channel_multiplier=0,
                           allow_small_or_imprecise_dtypes=True)
            nc.gpsimd.iota(pg.edge1[:, :], [[1, EC]], base=1, channel_multiplier=EC,
                           allow_small_or_imprecise_dtypes=True).then_inc(sem["iota_done"], 1)

        @block.scalar
        def _(act):
            act.wait_ge(sem["ints_in"], 48)
            act.wait_ge(sem["record_in"], 16)
            for n, at in enumerate((SRC, DST, TYPE)):
                nc.scalar.copy(record[:, :, at], ints[:, n, :]).then_inc(sem["record_built"], 1)

        @block.tensor
        def _(pe):
            pe.wait_ge(sem["rows_counted"], 1)
            nc.tensor.matmul(row_ps[0:EP, 0:NB], pg.before[0:EP, 0:EP], in_row[:, :], start=True, stop=True)
            nc.tensor.matmul(row_ps[:, 8:8 + NB], pg.ones[0:EP, :], in_row[:, :],
                             start=True, stop=True).then_inc(sem["rows_summed"], 1)

        @block.vector
        def _(dve):
            done = [0]

            def link(ins):
                done[0] += 1
                ins.then_inc(sem["chain"], 1)
                dve.wait_ge(sem["chain"], done[0])

            nc.vector.memset(zero[:, :], 0.0)
            dve.wait_ge(sem["dst_in"], 16)
            link(nc.vector.tensor_copy(dst[:, :], dst_i[:, :]))
            link(nc.vector.tensor_scalar(block_of[:, :], dst[:, :], float(BN), None, ALU.is_ge))
            for b in range(2, NB):
                link(nc.vector.scalar_tensor_tensor(out=block_of[:, :], in0=dst[:, :], scalar=float(BN * b),
                                                    in1=block_of[:, :], op0=ALU.is_ge, op1=ALU.add))
            for b in range(NB):
                last = nc.vector.tensor_scalar(mine[:, b, :], block_of[:, :], float(b), None, ALU.is_equal)
            link(last)
            for b in range(NB):
                last = nc.vector.tensor_tensor_scan(out=rank[:, b, :], data0=mine[:, b, :], data1=zero[:, :],
                                                    initial=0.0, op0=ALU.add, op1=ALU.add)
            link(last)
            nc.vector.tensor_copy(in_row[:, :], rank[:, :, EC - 1]).then_inc(sem["rows_counted"], 1)
            dve.wait_ge(sem["rows_summed"], 1)
            dve.wait_ge(sem["iota_done"], 1)
            link(nc.vector.tensor_copy(total[:, :], row_ps[:, 8:8 + NB]))
            for b in range(NB):
                link(nc.vector.tensor_scalar(full[:, :], group_edge[:, :], total[:, b:b + 1], 0.0, ALU.is_lt,
                                             ALU.add, accum_out=groups[:, b:b + 1]))
            link(nc.vector.memset(first_group[:, 0:1], 0.0))
            for b in range(NB):
                link(nc.vector.tensor_tensor(first_group[:, b + 1:b + 2], first_group[:, b:b + 1],
                                             groups[:, b:b + 1], ALU.add))
            link(nc.vector.tensor_scalar(group_blk[:, :], group_no[:, :], first_group[:, 1:2], None, ALU.is_ge))
            for b in range(2, NB):
                link(nc.vector.scalar_tensor_tensor(out=group_blk[:, :], in0=group_no[:, :],
                                                    scalar=first_group[:, b:b + 1], in1=group_blk[:, :],
                                                    op0=ALU.is_ge, op1=ALU.add))
            nc.vector.tensor_copy(pg.block_of_group[:, :], group_blk[0:1, :])
            for k in range(TG):
                nc.vector.tensor_copy(pg.block_of_tile[:, :].rearrange("p (g k) -> p g k", k=TG)[:, :, k],
                                      group_blk[:, :])
            link(nc.vector.scalar_tensor_tensor(out=shift[:, :], in0=first_group[0:EP, 0:NB], scalar=float(SG),
                                                in1=row_ps[0:EP, 0:NB], op0=ALU.mult, op1=ALU.add))
            for b in range(NB):
                last = nc.vector.scalar_tensor_tensor(out=rank[:, b, :], in0=rank[:, b, :], scalar=shift[:, b:b + 1],
                                                      in1=mine[:, b, :], op0=ALU.add, op1=ALU.mult)
            link(last)
            link(nc.vector.tensor_scalar(slot[:, :], rank[:, 0, :], 1.0, None, ALU.subtract))
            for b in range(1, NB):
                link(nc.vector.tensor_tensor(slot[:, :], slot[:, :], rank[:, b, :], ALU.add))
            link(nc.vector.tensor_copy(slot_i[:, :], slot[:, :]))
            nc.vector.tensor_scalar(lane_i[:, :], slot_i[:, :], P - 1, None, ALU.bitwise_and)
            link(nc.vector.tensor_scalar(tile_i[:, :], slot_i[:, :], 7, None, ALU.arith_shift_right))
            nc.vector.tensor_copy(pg.lane[:, :], lane_i[:, :])
            nc.vector.tensor_copy(pg.tile[:, :], tile_i[:, :])


def order_edges(pg):
    nc = pg.nc
    pg.edge_no = pg.sb("edge_no", [P, NT], U32)
    pg.filled = pg.sb("filled", [P, NT])
    with ExitStack() as ctx:
        lane_hot = pg.sb("lane_hot", [EP, 4, P], ctx=ctx)
        tile_edge = pg.sb("tile_edge", [EP, 4, NT], ctx=ctx)
        edge_f = pg.sb("edge_f", [P, NT], ctx=ctx)
        slots_ps = ctx.enter_context(nc.psum_tensor("slots_ps", [P, 512], FP32))
        hot, free, zeroed, placed, edge_sem = (ctx.enter_context(nc.semaphore(n)) for n in
                                       ("hot_ready", "hot_free", "slots_zeroed", "placed", "edge_chain"))
        block = ctx.enter_context(nc.Block())

        @block.vector
        def _(dve):
            with dve.Fori(0, EC // 4) as i:
                for s in range(4):
                    dve.wait_ge(free, 4 * i + s + 1)
                    j = 4 * i + s
                    nc.vector.tensor_scalar(lane_hot[:, s, :], pg.iota_free[0:EP, 0:P], pg.lane[:, bass.ds(j, 1)],
                                            None, ALU.is_equal)
                    nc.vector.tensor_scalar(tile_edge[:, s, :], pg.iota_free[0:EP, :], pg.tile[:, bass.ds(j, 1)],
                                            pg.edge1[:, bass.ds(j, 1)], ALU.is_equal, ALU.mult).then_inc(hot, 1)
            dve.wait_ge(placed, 1)
            nc.vector.tensor_scalar(pg.filled[:, :], slots_ps[:, 0:NT], 0.0, None, ALU.is_gt)
            nc.vector.tensor_scalar(edge_f[:, :], slots_ps[:, 0:NT], -1.0, 0.0, ALU.add, ALU.max).then_inc(edge_sem, 1)
            dve.wait_ge(edge_sem, 1)
            nc.vector.tensor_copy(pg.edge_no[:, :], edge_f[:, :])

        @block.gpsimd
        def _(pool):
            nc.gpsimd.memset(edge_f[:, :], 0.0).then_inc(zeroed, 1)

        @block.tensor
        def _(pe):
            pe.sem_inc(free, 4)
            pe.wait_ge(zeroed, 1)
            nc.tensor.matmul(slots_ps[:, 0:NT], pg.ident[:, :], edge_f[:, :], start=True, stop=False)
            with pe.Fori(0, EC // 4) as i:
                for s in range(4):
                    pe.wait_ge(hot, 4 * i + s + 1)
                    nc.tensor.matmul(slots_ps[:, 0:NT], lane_hot[:, s, :], tile_edge[:, s, :],
                                     start=False, stop=False).then_inc(free, 1)
            nc.tensor.matmul(slots_ps[:, 0:NT], pg.ident[:, :], edge_f[:, :], start=False, stop=True).then_inc(placed, 1)


def gather_loop(pg, pool, sems, table, rows, buffers, idx_tiles, width, ring=2):
    nc = pg.nc
    passed = sems["passed"]
    idx_copied, free, arrived = sems["idx_copied"], sems["gather_free"], sems["arrived"]
    with pool.Fori(0, NG // ring) as i:
        for h in range(ring):
            pool.wait_ge(free, (ring * i + h + 1) * TG)
            pool.sem_inc(passed, 1)
            nc.gpsimd.tensor_copy(idx_tiles[:, h, :], rows[:, bass.ds((ring * i + h) * TG, TG)]).then_inc(idx_copied, 1)
            pool.wait_ge(idx_copied, ring * i + h + 1)
            pool.sem_inc(passed, 1)
            for k in range(TG):
                b = h * TG + k
                nc.gpsimd.indirect_dma_start(
                    out=buffers[:, b, 0:width], out_offset=None, in_=table,
                    in_offset=bass.IndirectOffsetOnAxis(ap=idx_tiles[:, h, k:k + 1], axis=0)).then_inc(arrived[b], 16)


def gather_sems(pg, ctx, tag, ring=2):
    nc = pg.nc
    sems = {n: ctx.enter_context(nc.semaphore(f"{tag}_{n}")) for n in ("idx_copied", "gather_free", "passed")}
    sems["arrived"] = pg.arrived
    sems["before"] = list(pg.landed)
    for b in range(ring * TG):
        pg.landed[b] += 16 * (NG // ring)
    return sems


def fetch_records(pg):
    nc = pg.nc
    REST = RECORD - SMALL
    pg.record = pg.sb("slot_record", [P, NT, REST])
    pg.src_row = pg.sb("src_row", [P, NT], U32)
    pg.rel_row = pg.sb("rel_row", [P, NT], U32)
    pg.dst_in_block = pg.sb("dst_in_block", [P, NT])
    pg.attrT = nc.dram_tensor("attrT", [NG, A8, SG], BF16).ap()
    pg.attr_restT = nc.dram_tensor("attr_restT", [NG, A8, SG], BF16).ap()
    pg.attr8T = nc.dram_tensor("attr8T", [NG, SMALL - A8, SG], FP32).ap()
    with ExitStack() as ctx:
        landing = pg.sb("landing", [P, 2 * TG, RECORD], ctx=ctx)
        idx = pg.sb("idx", [P, 2, TG], U32, ctx)
        turned = pg.sb("attr_rows", [SMALL, 2, SG], ctx=ctx)
        high = pg.sb("attr_high", [A8, 2, SG], BF16, ctx)
        low = pg.sb("attr_low", [A8, 2, SG], BF16, ctx)
        t0 = pg.sb("t0", [P, NT], ctx=ctx)
        t1 = pg.sb("t1", [P, NT], ctx=ctx)
        ps = [ctx.enter_context(nc.psum_tensor(f"rec_ps{h}", [P, SG], FP32)) for h in range(2)]
        sems = gather_sems(pg, ctx, "rec")
        chain, kept, made, copied, rounded, halved = (ctx.enter_context(nc.semaphore(n)) for n in
                                     ("rec_chain", "rec_kept", "rec_made", "rec_copied",
                                      "rec_rounded", "rec_halved"))
        stored = [ctx.enter_context(nc.semaphore(f"rec_stored{h}")) for h in range(2)]
        block = ctx.enter_context(nc.Block())

        @block.gpsimd
        def _(pool):
            gather_loop(pg, pool, sems, pg.records, pg.edge_no, landing, idx, RECORD)

        @block.tensor
        def _(pe):
            pe.sem_inc(sems["gather_free"], 2 * TG)
            pe.sem_inc(copied, 2)
            with pe.Fori(0, NG // 2) as i:
                for h in range(2):
                    pe.wait_ge(copied, 2 * i + h + 1)
                    for k in range(TG):
                        pe.wait_ge(sems["arrived"][h * TG + k], sems["before"][h * TG + k] + 16 * i + 16)
                        nc.tensor.transpose(ps[h][0:SMALL, k * P:(k + 1) * P], landing[:, h * TG + k, 0:SMALL],
                                            pg.ident[:, :]).then_inc(made, 1)
                    pe.wait_ge(made, (2 * i + h + 1) * TG)
                    pe.wait_ge(kept, (2 * i + h + 1) * TG)
                    pe.sem_inc(sems["gather_free"], TG)

        @block.scalar
        def _(act):
            act.sem_inc(stored[0], 48)
            act.sem_inc(stored[1], 48)
            with act.Fori(0, NG // 2) as i:
                for h in range(2):
                    act.wait_ge(stored[h], 48 * i + 48)
                    act.wait_ge(made, (2 * i + h + 1) * TG)
                    nc.scalar.copy(turned[:, h, :], ps[h][0:SMALL, :]).then_inc(copied, 1)
                    act.wait_ge(copied, 2 * i + h + 3)
                    nc.scalar.copy(high[:, h, :], turned[0:A8, h, :]).then_inc(rounded, 1)

        @block.sync
        def _(sp):
            with sp.Fori(0, NG // 2) as i:
                for h in range(2):
                    sp.wait_ge(halved, 2 * i + h + 1)
                    at = bass.ds(2 * i + h, 1)
                    for to, rows in ((pg.attrT, high[:, h, :]), (pg.attr_restT, low[:, h, :]),
                                     (pg.attr8T, turned[A8:SMALL, h, :])):
                        sp.dma_start(to[at, :, :].rearrange("a r e -> (a r) e"), rows).then_inc(stored[h], 16)
            for h in range(2):
                sp.wait_ge(stored[h], 48 * (NG // 2) + 48)

        @block.vector
        def _(dve):
            done = [0]

            def link(ins):
                done[0] += 1
                ins.then_inc(chain, 1)
                dve.wait_ge(chain, done[0])

            with dve.Fori(0, NG // 2) as i:
                for b in range(2 * TG):
                    dve.wait_ge(sems["arrived"][b], sems["before"][b] + 16 * i + 16)
                    nc.vector.tensor_copy(pg.record[:, bass.ds(i * 2 * TG + b, 1), :].rearrange("p a r -> p (a r)"),
                                          landing[:, b, SMALL:RECORD]).then_inc(kept, 1)
                    if b % TG == TG - 1:
                        h = b // TG
                        dve.wait_ge(rounded, 2 * i + h + 1)
                        nc.vector.tensor_tensor(low[:, h, :], turned[0:A8, h, :], high[:, h, :],
                                                ALU.subtract).then_inc(halved, 1)
            dve.wait_ge(kept, NT)
            src, dst, rel = (pg.record[:, :, at - SMALL] for at in (SRC, DST, TYPE))
            nc.vector.tensor_copy(pg.src_row[:, :], src)
            link(nc.vector.scalar_tensor_tensor(out=t0[:, :], in0=rel, scalar=float(NODES),
                                                in1=src, op0=ALU.mult, op1=ALU.add))
            nc.vector.tensor_copy(pg.rel_row[:, :], t0[:, :])
            link(nc.vector.scalar_tensor_tensor(out=t1[:, :], in0=pg.block_of_tile[:, :], scalar=-float(BN),
                                                in1=dst, op0=ALU.mult, op1=ALU.add))
            link(nc.vector.scalar_tensor_tensor(out=t1[:, :], in0=t1[:, :], scalar=1.0, in1=pg.filled[:, :],
                                                op0=ALU.add, op1=ALU.mult))
            nc.vector.tensor_scalar(pg.dst_in_block[:, :], t1[:, :], -1.0, None, ALU.add)


def load_nodes(pg):
    nc = pg.nc
    pg.x = pg.sb("x", [BN, NB, D])
    pg.h = pg.sb("h", [BN, NB, D])
    pg.hT = pg.sb("hT", [P, D // P, NODES])
    with nc.semaphore("x_in") as x_in, nc.Block() as block:
        @block.sync
        def _(sp):
            sp.dma_start(pg.x[:, :, :], pg.inp["x"].rearrange("(b p) d -> p b d", p=BN)).then_inc(x_in, 16)
            sp.wait_ge(x_in, 16)


def normalize(pg, tag, h_table=None):
    nc = pg.nc
    with ExitStack() as ctx:
        stats = pg.sb(f"{tag}_stats", [BN, NB, 6], ctx=ctx)
        mv = pg.sb(f"{tag}_mv", [BN, NB, 2], ctx=ctx)
        sd = pg.sb(f"{tag}_sd", [BN, NB], ctx=ctx)
        rs = pg.sb(f"{tag}_rs", [BN, NB], ctx=ctx)
        nmr = pg.sb(f"{tag}_nmr", [BN, NB], ctx=ctx)
        ps = [ctx.enter_context(nc.psum_tensor(f"{tag}_ps{i}", [P, D // P, P], FP32)) for i in range(2)]
        chain, var, root, scaled, normed, turned, taken, stored = (
            ctx.enter_context(nc.semaphore(f"{tag}_{n}"))
            for n in ("chain", "var", "root", "scaled", "normed", "turned", "taken", "stored"))
        block = ctx.enter_context(nc.Block())

        @block.vector
        def _(dve):
            for b in range(NB):
                last = nc.vector.bn_stats(out=stats[:, b, :], in_=pg.x[:, b, :])
            last.then_inc(chain, 1)
            dve.wait_ge(chain, 1)
            for b in range(NB):
                last = nc.vector.bn_aggr(out=mv[:, b, :], in_=stats[:, b, :])
            last.then_inc(chain, 1)
            dve.wait_ge(chain, 2)
            nc.vector.tensor_scalar(sd[:, :], mv[:, :, 1], EPS, None, ALU.add).then_inc(var, 1)
            dve.wait_ge(root, 1)
            nc.vector.reciprocal(rs[:, :], sd[:, :]).then_inc(chain, 1)
            dve.wait_ge(chain, 3)
            nc.vector.scalar_tensor_tensor(out=nmr[:, :], in0=mv[:, :, 0], scalar=-1.0, in1=rs[:, :],
                                           op0=ALU.mult, op1=ALU.mult).then_inc(scaled, 1)
            for b in range(NB):
                dve.wait_ge(turned, b + 1)
                nc.vector.tensor_copy(pg.hT[:, :, b * BN:(b + 1) * BN], ps[b % 2][:, :, 0:BN]).then_inc(taken, 1)

        @block.scalar
        def _(act):
            act.wait_ge(var, 1)
            nc.scalar.sqrt(sd[:, :], sd[:, :]).then_inc(root, 1)
            act.wait_ge(scaled, 1)
            for b in range(NB):
                nc.scalar.activation(pg.h[:, b, :], pg.x[:, b, :], ACT.Relu, bias=nmr[:, b:b + 1],
                                     scale=rs[:, b:b + 1]).then_inc(normed, 1)

        @block.sync
        def _(sp):
            if h_table is not None:
                sp.wait_ge(normed, NB)
                sp.dma_start(h_table.rearrange("(b p) d -> p b d", p=BN), pg.h[:, :, :]).then_inc(stored, 16)
                sp.wait_ge(stored, 16)

        @block.tensor
        def _(pe):
            for b in range(NB):
                pe.wait_ge(normed, b + 1)
                if b >= 2:
                    pe.wait_ge(taken, b - 1)
                for f in range(D // P):
                    last = nc.tensor.transpose(ps[b % 2][:, f, 0:BN], pg.h[:, b, f * P:(f + 1) * P],
                                               pg.ident[0:BN, 0:BN])
                last.then_inc(turned, 1)


def transpose_nodes(pg, tag, src, dst, blocks_of_columns):
    nc = pg.nc
    with ExitStack() as ctx:
        ps = [ctx.enter_context(nc.psum_tensor(f"{tag}_ps{i}", [P, 4, P], FP32)) for i in range(2)]
        turned, taken = (ctx.enter_context(nc.semaphore(f"{tag}_{n}")) for n in ("turned", "taken"))
        block = ctx.enter_context(nc.Block())
        steps = [(b, f0) for b in range(NB) for f0 in range(0, blocks_of_columns, 4)]

        @block.tensor
        def _(pe):
            for n, (b, f0) in enumerate(steps):
                if n >= 2:
                    pe.wait_ge(taken, n - 1)
                for f in range(4):
                    last = nc.tensor.transpose(ps[n % 2][:, f, 0:BN], src[:, b, (f0 + f) * P:(f0 + f + 1) * P],
                                               pg.ident[0:BN, 0:BN])
                last.then_inc(turned, 1)

        @block.vector
        def _(dve):
            for n, (b, f0) in enumerate(steps):
                dve.wait_ge(turned, n + 1)
                nc.vector.tensor_copy(dst[:, f0:f0 + 4, b * BN:(b + 1) * BN], ps[n % 2][:, :, 0:BN]).then_inc(taken, 1)


def segment_sum(pg, tag, table, rows, total, weight=None, count=None):
    nc = pg.nc
    with ExitStack() as ctx:
        got = pg.sb(f"{tag}_got", [P, RING * TG, D], ctx=ctx)
        idx = pg.sb(f"{tag}_idx", [P, RING, TG], U32, ctx)
        hot = pg.sb(f"{tag}_hot", [P, RING * TG, BN], ctx=ctx)
        sum_ps = [ctx.enter_context(nc.psum_tensor(f"{tag}_sum{h}", [P, D], FP32)) for h in range(2)]
        cnt_ps = [ctx.enter_context(nc.psum_tensor(f"{tag}_cnt{h}", [P, D], FP32)) for h in range(2)]
        sems = gather_sems(pg, ctx, tag, RING)
        hot_ready, added, cleared = (ctx.enter_context(nc.semaphore(f"{tag}_{n}"))
                                     for n in ("hot_ready", "added", "cleared"))
        tile_done = sems["gather_free"]
        block = ctx.enter_context(nc.Block())

        @block.gpsimd
        def _(pool):
            nc.gpsimd.memset(total[:, :, :], 0.0).then_inc(cleared, 1)
            if count is not None:
                nc.gpsimd.memset(count[:, :], 0.0).then_inc(cleared, 1)
            gather_loop(pg, pool, sems, table, rows, got, idx, D, RING)

        @block.tensor
        def _(pe):
            pe.sem_inc(tile_done, RING * TG)
            with pe.Fori(0, NG // RING) as i:
                for h in range(RING):
                    g = RING * i + h
                    pe.wait_ge(added, g + 1)
                    for k in range(TG):
                        b = h * TG + k
                        pe.wait_ge(sems["arrived"][b], sems["before"][b] + 16 * i + 16)
                        pe.wait_ge(hot_ready, g * TG + k + 1)
                        if count is not None:
                            nc.tensor.matmul(cnt_ps[h % 2][0:BN, 0:1], hot[:, b, :], pg.ones[:, 0:1],
                                             start=(k == 0), stop=(k == TG - 1))
                        nc.tensor.matmul(sum_ps[h % 2][0:BN, :], hot[:, b, :], got[:, b, :],
                                         start=(k == 0), stop=(k == TG - 1)).then_inc(tile_done, 1)

        @block.vector
        def _(dve):
            def one_hots(g, h):
                for k in range(TG):
                    b, t = h * TG + k, g * TG + k
                    dve.wait_ge(tile_done, t + 1)
                    if weight is None:
                        ins = nc.vector.tensor_scalar(hot[:, b, :], pg.iota_free[:, 0:BN],
                                                      pg.dst_in_block[:, bass.ds(t, 1)], None, ALU.is_equal)
                    else:
                        ins = nc.vector.tensor_scalar(hot[:, b, :], pg.iota_free[:, 0:BN],
                                                      pg.dst_in_block[:, bass.ds(t, 1)], weight(t),
                                                      ALU.is_equal, ALU.mult)
                    ins.then_inc(hot_ready, 1)

            def add(g, h):
                at = nc.vector.value_load(pg.block_of_group[0:1, bass.ds(g, 1)], min_val=0, max_val=NB - 1)
                dve.wait_ge(tile_done, (g + 1) * TG + RING * TG)
                dve.wait_ge(added, g + 2)
                into = total[:, bass.ds(at, 1), :].rearrange("p a d -> p (a d)")
                if count is not None:
                    nc.vector.tensor_tensor(count[:, bass.ds(at, 1)], count[:, bass.ds(at, 1)],
                                            cnt_ps[h % 2][0:BN, 0:1], ALU.add)
                nc.vector.tensor_tensor(into, into, sum_ps[h % 2][0:BN, :], ALU.add).then_inc(added, 1)

            dve.sem_inc(added, 2)
            dve.wait_ge(cleared, 1 if count is None else 2)
            for h in range(RING - 1):
                one_hots(h, h)
            with dve.Fori(0, NG // RING - 1) as i:
                for h in range(RING):
                    one_hots(RING * i + h + RING - 1, (h + RING - 1) % RING)
                    add(RING * i + h, h)
            for h in range(RING):
                if h == 0:
                    one_hots(NG - 1, RING - 1)
                add(NG - RING + h, h)


def row_on_all(row, partitions):
    return row.rearrange("(a n) -> a n", a=1).broadcast_to([partitions, row.shape[0]])


def weight_rows(w):
    return w.rearrange("(f p) n -> p f n", p=P)


def node_stage(pg, tag, loads, products, finish, scalar_finish=None):
    nc = pg.nc
    with ExitStack() as ctx:
        ps = [ctx.enter_context(nc.psum_tensor(f"{tag}_ps{i}", [P, D], FP32)) for i in range(2)]
        loaded, made, taken, chain, half, given = (ctx.enter_context(nc.semaphore(f"{tag}_{n}"))
                                                   for n in ("loaded", "made", "taken", "chain", "half", "given"))
        block = ctx.enter_context(nc.Block())

        @block.sync
        def _(sp):
            for to, src in loads:
                sp.dma_start(to, src).then_inc(loaded, 16)
            sp.wait_ge(loaded, 16 * len(loads))

        @block.tensor
        def _(pe):
            pe.wait_ge(loaded, 16 * len(loads))
            for b in range(NB):
                if b >= 2:
                    pe.wait_ge(taken, b - 1)
                products(b, ps[b % 2]).then_inc(made, 1)

        @block.vector
        def _(dve):
            done = [0]

            def link(ins):
                done[0] += 1
                ins.then_inc(chain, 1)
                dve.wait_ge(chain, done[0])

            dve.wait_ge(loaded, 16 * len(loads))
            for b in range(NB):
                dve.wait_ge(made, b + 1)
                finish(b, ps[b % 2][0:BN, :], link).then_inc(taken, 1)


def accumulate(nc, out, pairs):
    for n, (lhsT, rhs) in enumerate(pairs):
        last = nc.tensor.matmul(out, lhsT, rhs, start=(n == 0), stop=(n == len(pairs) - 1))
    return last


def nodes_of(b):
    return slice(b * BN, (b + 1) * BN)


def layer0(pg):
    nc = pg.nc
    pg.h_table = nc.dram_tensor("h_table", [NODES, D], FP32).ap()
    normalize(pg, "n0", pg.h_table)
    with ExitStack() as ctx:
        total = pg.sb("total0", [BN, NB, D], ctx=ctx)
        count = pg.sb("count0", [BN, NB], ctx=ctx)
        totalT = pg.sb("total0T", [P, 4, NODES], ctx=ctx)
        w = pg.sb("w0", [P, 8, D], ctx=ctx)
        bias = pg.sb("bias0", [BN, D], ctx=ctx)
        segment_sum(pg, "g0", pg.h_table, pg.src_row, total, count=count)
        with nc.semaphore("mean_chain") as chain, nc.Block() as block:
            @block.vector
            def _(dve):
                nc.vector.tensor_scalar(count[:, :], count[:, :], 1.0, None, ALU.max).then_inc(chain, 1)
                dve.wait_ge(chain, 1)
                nc.vector.reciprocal(count[:, :], count[:, :]).then_inc(chain, 1)
                dve.wait_ge(chain, 2)
                for b in range(NB):
                    nc.vector.tensor_scalar(total[:, b, :], total[:, b, :], count[:, b:b + 1], None, ALU.mult)
        transpose_nodes(pg, "t0", total, totalT, 4)

        def products(b, ps):
            return accumulate(nc, ps[0:BN, :], [(pg.hT[:, f, nodes_of(b)], w[:, f, :]) for f in range(4)]
                              + [(totalT[:, f, nodes_of(b)], w[:, 4 + f, :]) for f in range(4)])

        def finish(b, ps, link):
            link(nc.vector.tensor_tensor(pg.x[:, b, :], pg.x[:, b, :], ps, ALU.add))
            return nc.vector.tensor_tensor(pg.x[:, b, :], pg.x[:, b, :], bias[:, :], ALU.add)

        node_stage(pg, "w0s", [(w[:, :, :], weight_rows(pg.inp["L0_gnn_W"])),
                               (bias[:, :], row_on_all(pg.inp["L0_gnn_b"], BN))], products, finish)


def relation_tables(pg, tag, basis_in, comp_in, table):
    nc = pg.nc
    with ExitStack() as ctx:
        basis = pg.sb(f"{tag}_basis", [P, BASES, 4 * D], ctx=ctx)
        comp = pg.sb(f"{tag}_comp", [P, RELS * BASES], ctx=ctx)
        w = pg.sb(f"{tag}_w", [P, 2, 4 * D], ctx=ctx)
        rows = pg.sb(f"{tag}_rows", [BN, 2, NB, D], ctx=ctx)
        ps = [ctx.enter_context(nc.psum_tensor(f"{tag}_ps{i}", [P, D], FP32)) for i in range(2)]
        loaded, mixed, chain, used, made, taken = (ctx.enter_context(nc.semaphore(f"{tag}_{n}")) for n in
                                                   ("loaded", "mixed", "chain", "used", "made", "taken"))
        stored = [ctx.enter_context(nc.semaphore(f"{tag}_stored{i}")) for i in range(2)]
        block = ctx.enter_context(nc.Block())

        @block.sync
        def _(sp):
            sp.dma_start(comp[:, :], row_on_all(comp_in.rearrange("r b -> (r b)"), P)).then_inc(loaded, 16)
            for k in range(BASES):
                sp.dma_start(basis[:, k, :].rearrange("p (f n) -> p f n", f=4),
                             weight_rows(basis_in[k, :, :])).then_inc(loaded, 16)
            for r in range(RELS):
                sp.wait_ge(taken, NB * (r + 1))
                sp.dma_start(table[r * NODES:(r + 1) * NODES, :].rearrange("(b p) d -> p b d", p=BN),
                             rows[:, r % 2, :, :]).then_inc(stored[r % 2], 16)
            for n in range(2):
                sp.wait_ge(stored[n], 16 * RELS // 2)

        @block.vector
        def _(dve):
            dve.wait_ge(loaded, 16 * (BASES + 1))
            for r in range(RELS):
                if r >= 2:
                    dve.wait_ge(used, r - 1)
                for k in range(BASES):
                    c = comp[:, r * BASES + k:r * BASES + k + 1]
                    if k == 0:
                        ins = nc.vector.tensor_scalar(w[:, r % 2, :], basis[:, k, :], c, None, ALU.mult)
                    else:
                        ins = nc.vector.scalar_tensor_tensor(out=w[:, r % 2, :], in0=basis[:, k, :], scalar=c,
                                                             in1=w[:, r % 2, :], op0=ALU.mult, op1=ALU.add)
                    ins.then_inc(chain, 1)
                    dve.wait_ge(chain, BASES * r + k + 1)
                dve.sem_inc(mixed, 1)

        @block.tensor
        def _(pe):
            for r in range(RELS):
                pe.wait_ge(mixed, r + 1)
                for b in range(NB):
                    n = r * NB + b
                    if n >= 2:
                        pe.wait_ge(taken, n - 1)
                    accumulate(nc, ps[n % 2][0:BN, :],
                               [(pg.hT[:, f, nodes_of(b)], w[:, r % 2, f * D:(f + 1) * D])
                                for f in range(4)]).then_inc(made, 1)
                pe.wait_ge(made, (r + 1) * NB)
                pe.sem_inc(used, 1)

        @block.scalar
        def _(act):
            for r in range(RELS):
                if r >= 2:
                    act.wait_ge(stored[r % 2], 16 * (r // 2))
                for b in range(NB):
                    act.wait_ge(made, r * NB + b + 1)
                    nc.scalar.copy(rows[:, r % 2, b, :], ps[(r * NB + b) % 2][0:BN, :]).then_inc(taken, 1)


def layer1(pg):
    nc = pg.nc
    rel_table = nc.dram_tensor("rel_table", [RELS * NODES, D], FP32).ap()
    normalize(pg, "n1")
    for c in range(2):
        relation_tables(pg, f"rt{c}", pg.inp[f"L1_gnn_basis{c}"], pg.inp[f"L1_gnn_comp{c}"], rel_table)
        with ExitStack() as ctx:
            total = pg.sb(f"total1{c}", [BN, NB, D], ctx=ctx)
            loop_w = pg.sb(f"loop{c}", [P, 4, D], ctx=ctx)
            bias = pg.sb(f"bias1{c}", [BN, D], ctx=ctx)
            segment_sum(pg, f"g1{c}", rel_table, pg.rel_row, total,
                        weight=lambda t: pg.record[:, bass.ds(t, 1), WEIGHT])

            def products(b, ps):
                return accumulate(nc, ps[0:BN, :], [(pg.hT[:, f, nodes_of(b)], loop_w[:, f, :]) for f in range(4)])

            def finish(b, ps, link):
                link(nc.vector.tensor_tensor(total[:, b, :], total[:, b, :], ps, ALU.add))
                link(nc.vector.tensor_tensor(total[:, b, :], total[:, b, :], bias[:, :], ALU.add))
                if c == 0:
                    return nc.vector.tensor_scalar(pg.h[:, b, :], total[:, b, :], 0.0, None, ALU.max)
                return nc.vector.tensor_tensor(pg.x[:, b, :], pg.x[:, b, :], total[:, b, :], ALU.add)

            node_stage(pg, f"lw{c}", [(loop_w[:, :, :], weight_rows(pg.inp[f"L1_gnn_loop{c}"])),
                                      (bias[:, :], row_on_all(pg.inp[f"L1_gnn_bias{c}"], BN))], products, finish)
        if c == 0:
            transpose_nodes(pg, "t1", pg.h, pg.hT, 4)


def four_at_a_time(eng, body):
    for g in range(RING):
        body(g, g, g)
    with eng.Fori(1, NG // RING - 1) as i:
        for r in range(RING):
            body(RING * i + r, r, RING)
    for r in range(RING):
        body(NG - RING + r, r, NG - RING + r)


def hot_tiles(pg, dve, hot, hot_free, hot_ready, g, h):
    for k in range(TG):
        t = g * TG + k
        dve.wait_ge(hot_free, t + 1)
        pg.nc.vector.tensor_scalar(hot[:, h * TG + k, :], pg.iota_free[:, 0:BN],
                                   pg.dst_in_block[:, bass.ds(t, 1)], None, ALU.is_equal).then_inc(hot_ready, 1)


def message_pass(pg, tag, tableU, total):
    nc = pg.nc
    M = 8 * MUL
    LAST = NG - 1
    with ExitStack() as ctx:
        got = pg.sb("u_got", [P, 2 * TG, D], ctx=ctx)
        idx = pg.sb("u_idx", [P, 2, TG], U32, ctx)
        hot = pg.sb("u_hot", [P, 2 * TG, BN], ctx=ctx)
        w1 = pg.sb("u_w1", [8, HID], ctx=ctx)
        w2 = pg.sb("u_w2", [HID, HID], ctx=ctx)
        w3 = pg.sb("u_w3", [HID, HID], ctx=ctx)
        w4 = pg.sb("u_w4", [HID, D], ctx=ctx)
        attrT = pg.sb("u_attrT", [8, 2, SG], ctx=ctx)
        hid = [pg.sb(f"u_hid{n}", [HID, SG], ctx=ctx) for n in range(2)]
        hid3 = pg.sb("u_hid3", [HID, 2, SG], ctx=ctx)
        t2 = pg.sb("u_t2", [P, 2, MUL], ctx=ctx)
        q = pg.sb("u_q", [P, 2, MUL], ctx=ctx)
        msg = pg.sb("u_msg", [P, 2, M], ctx=ctx)
        mlp_ps = ctx.enter_context(nc.psum_tensor("u_mlp_ps", [P, SG], FP32))
        tp_ps = [ctx.enter_context(nc.psum_tensor(f"u_tp_ps{n}", [P, D], FP32)) for n in range(2)]
        sum_ps = [ctx.enter_context(nc.psum_tensor(f"u_sum_ps{n}", [P, M], FP32)) for n in range(2)]
        sems = gather_sems(pg, ctx, "u")
        (loaded, cleared, hot_ready, hot_free, attr_free, layer_made, layer_done, tp_ready, t2_ready,
         q_chain, msg_dve, msg_act, added, passed) = (ctx.enter_context(nc.semaphore(f"u_{n}")) for n in (
             "loaded", "cleared", "hot_ready", "hot_free", "attr_free", "layer_made", "layer_done",
             "tp_ready", "t2_ready", "q_chain", "msg_dve", "msg_act", "added", "pe_passed"))
        attr_in = [ctx.enter_context(nc.semaphore(f"u_attr_in{h}")) for h in range(2)]
        block = ctx.enter_context(nc.Block())

        @block.sync
        def _(sp):
            for to, src in ((w1, "W_mlp1"), (w2, "W_mlp2"), (w3, "W_mlp3"), (w4, "W_mlp4")):
                sp.dma_start(to[:, :], pg.inp[f"L2_gnn_{src}"]).then_inc(loaded, 16)
            sp.sem_inc(attr_free, 2)
            with sp.Fori(0, NG // 2) as i:
                for h in range(2):
                    sp.wait_ge(attr_free, 2 * i + h + 1)
                    sp.dma_start(attrT[:, h, :], pg.attr8T[bass.ds(2 * i + h, 1), :, :]
                                 .rearrange("a r e -> (a r) e")).then_inc(attr_in[h], 16)

        @block.gpsimd
        def _(pool):
            nc.gpsimd.memset(total[:, :, :], 0.0).then_inc(cleared, 1)
            gather_loop(pg, pool, sems, tableU, pg.src_row, got, idx, D)

        @block.tensor
        def _(pe):
            def layer(g, h, n):
                if n == 0:
                    pe.wait_ge(attr_in[h], (g - h) * 8 + 16)
                else:
                    pe.wait_ge(layer_done, 3 * g + n)
                    pe.sem_inc(passed, 1)
                lhsT, rhs = ((w1, attrT[:, h, :]), (w2, hid[0][:, :]), (w3, hid[1][:, :]))[n]
                nc.tensor.matmul(mlp_ps[0:HID, :], lhsT[:, :], rhs, start=True, stop=True).then_inc(layer_made, 1)
                if n == 0:
                    pe.wait_ge(layer_made, 3 * g + 1)
                    pe.sem_inc(attr_free, 1)

            def path_weights(g, h, k):
                nc.tensor.matmul(tp_ps[k % 2][:, :], hid3[:, h, k * P:(k + 1) * P], w4[:, :],
                                 start=True, stop=True).then_inc(tp_ready, 1)

            def scatter(g, h, k):
                t = g * TG + k
                pe.wait_ge(msg_dve, t + 1)
                pe.wait_ge(msg_act, t + 2)
                if k == 0:
                    pe.wait_ge(added, g + 1)
                nc.tensor.matmul(sum_ps[h][0:BN, 0:D], hot[:, h * TG + k, :], msg[:, k % 2, 0:D],
                                 start=(k == 0), stop=(k == TG - 1))
                nc.tensor.matmul(sum_ps[h][0:BN, D:M], hot[:, h * TG + k, :], msg[:, k % 2, D:M],
                                 start=(k == 0), stop=(k == TG - 1)).then_inc(hot_free, 1)

            def body(g, r, at):
                h = r % 2
                for k in range(TG):
                    if k < 3 and at < LAST:
                        layer(g + 1, 1 - h, k)
                    if k < TG - 1:
                        path_weights(g, h, k + 1)
                    elif at < LAST:
                        pe.wait_ge(layer_done, 3 * g + 6)
                        path_weights(g + 1, 1 - h, 0)
                    scatter(g, h, k)

            pe.sem_inc(hot_free, 2 * TG)
            pe.wait_ge(loaded, 64)
            for n in range(3):
                layer(0, 0, n)
            pe.wait_ge(hot_ready, 2 * TG)
            pe.wait_ge(layer_done, 3)
            path_weights(0, 0, 0)
            four_at_a_time(pe, body)

        @block.scalar
        def _(act):
            def layer(g, h, n):
                act.wait_ge(layer_made, 3 * g + n + 1)
                scale = 1.0 / np.sqrt(8.0) if n == 0 else SILU_2MOM / np.sqrt(float(HID))
                to = (hid[0][:, :], hid[1][:, :], hid3[:, h, :])[n]
                nc.scalar.activation(to, mlp_ps[0:HID, :], ACT.Silu, scale=float(scale)).then_inc(layer_done, 1)

            def vector_paths(g, h, k):
                t = g * TG + k
                act.wait_ge(t2_ready, t + 1)
                for m in range(3):
                    last = nc.scalar.activation(msg[:, k % 2, (2 + m) * MUL:(3 + m) * MUL], t2[:, k % 2, :], ACT.Copy,
                                                scale=pg.record[:, bass.ds(t, 1), Y + 1 + m])
                last.then_inc(msg_act, 1)

            def body(g, r, at):
                for k in range(TG):
                    if k < 3 and at < LAST:
                        layer(g + 1, 1 - r % 2, k)
                    vector_paths(g, r % 2, k)

            act.sem_inc(msg_act, 1)
            for n in range(3):
                layer(0, 0, n)
            four_at_a_time(act, body)

        @block.vector
        def _(dve):
            def paths(g, h, k):
                t = g * TG + k
                b = h * TG + k
                y = [pg.record[:, bass.ds(t, 1), Y + m] for m in range(4)]
                tp = tp_ps[k % 2]
                s0, s1 = got[:, b, 0:MUL], [got[:, b, (1 + m) * MUL:(2 + m) * MUL] for m in range(3)]
                dve.wait_ge(sems["arrived"][b], sems["before"][b] + (g - h) * 8 + 16)
                dve.wait_ge(hot_free, g * TG + k - 1 + 2 * TG)
                nc.vector.tensor_scalar(q[:, k % 2, :], s1[0], y[1], None, ALU.mult).then_inc(q_chain, 1)
                dve.wait_ge(tp_ready, t + 1)
                dve.wait_ge(msg_act, t)
                nc.vector.tensor_tensor(t2[:, k % 2, :], tp[:, MUL:2 * MUL], s0, ALU.mult).then_inc(t2_ready, 1)
                nc.vector.scalar_tensor_tensor(out=msg[:, k % 2, 0:MUL], in0=tp[:, 0:MUL], scalar=y[0], in1=s0,
                                               op0=ALU.mult, op1=ALU.mult)
                dve.wait_ge(q_chain, 3 * t + 1)
                nc.vector.scalar_tensor_tensor(out=q[:, k % 2, :], in0=s1[1], scalar=y[2], in1=q[:, k % 2, :],
                                               op0=ALU.mult, op1=ALU.add).then_inc(q_chain, 1)
                nc.vector.scalar_tensor_tensor(
                    out=msg[:, k % 2, 5 * MUL:8 * MUL].rearrange("p (m u) -> p m u", m=3),
                    in0=tp[:, 2 * MUL:3 * MUL].rearrange("p (a u) -> p a u", a=1).broadcast_to([P, 3, MUL]),
                    scalar=y[0], in1=got[:, b, MUL:D].rearrange("p (m u) -> p m u", m=3),
                    op0=ALU.mult, op1=ALU.mult)
                dve.wait_ge(q_chain, 3 * t + 2)
                nc.vector.scalar_tensor_tensor(out=q[:, k % 2, :], in0=s1[2], scalar=y[3], in1=q[:, k % 2, :],
                                               op0=ALU.mult, op1=ALU.add).then_inc(q_chain, 1)
                dve.wait_ge(q_chain, 3 * t + 3)
                nc.vector.tensor_tensor(msg[:, k % 2, MUL:2 * MUL], tp[:, 3 * MUL:4 * MUL], q[:, k % 2, :],
                                        ALU.mult).then_inc(msg_dve, 1)
                if k == TG - 1:
                    dve.wait_ge(msg_dve, t + 1)
                    dve.sem_inc(sems["gather_free"], TG)

            def add(g, h):
                at = nc.vector.value_load(pg.block_of_group[0:1, bass.ds(g, 1)], min_val=0, max_val=NB - 1)
                dve.wait_ge(hot_free, (g + 1) * TG + 2 * TG)
                dve.wait_ge(added, g + 2)
                into = total[:, bass.ds(at, 1), :].rearrange("p a d -> p (a d)")
                nc.vector.tensor_tensor(into, into, sum_ps[h][0:BN, :], ALU.add).then_inc(added, 1)

            def body(g, r, at):
                h = r % 2
                for k in range(TG):
                    paths(g, h, k)
                    if k == 1 and at > 0:
                        add(g - 1, 1 - h)
                        if at < LAST:
                            hot_tiles(pg, dve, hot, hot_free, hot_ready, g + 1, 1 - h)

            dve.sem_inc(sems["gather_free"], 2 * TG)
            dve.sem_inc(added, 2)
            hot_tiles(pg, dve, hot, hot_free, hot_ready, 0, 0)
            hot_tiles(pg, dve, hot, hot_free, hot_ready, 1, 1)
            dve.wait_ge(cleared, 1)
            four_at_a_time(dve, body)
            add(LAST, LAST % 2)


def layer2(pg):
    nc = pg.nc
    normalize(pg, "n2")
    tableU = nc.dram_tensor("up_table", [NODES, D], FP32).ap()
    with ExitStack() as ctx:
        total = pg.sb("total2", [BN, NB, 8 * MUL], ctx=ctx)
        with ExitStack() as up:
            split = pg.sb("split", [BN, NB, D], ctx=up)
            splitT = pg.sb("splitT", [P, 4, NODES], ctx=up)
            w_up = pg.sb("w_up", [P, 2, MUL], ctx=up)
            rows = pg.sb("up_rows", [BN, NB, D], ctx=up)
            with nc.Block() as block:
                @block.vector
                def _(dve):
                    nc.vector.tensor_copy(split[:, :, 0:MUL], pg.h[:, :, 0:MUL])
                    for b in range(NB):
                        nc.vector.tensor_copy(split[:, b, MUL:D].rearrange("p (m u) -> p m u", m=3),
                                              pg.h[:, b, MUL:D].rearrange("p (u m) -> p m u", m=3))
            transpose_nodes(pg, "t2", split, splitT, 4)

            def products(b, ps):
                for f in range(4):
                    last = nc.tensor.matmul(ps[0:BN, f * MUL:(f + 1) * MUL], splitT[:, f, nodes_of(b)],
                                            w_up[:, min(f, 1), :], start=True, stop=True)
                return last

            node_stage(pg, "up", [(w_up[:, 0, :], pg.inp["L2_gnn_W_up0"]), (w_up[:, 1, :], pg.inp["L2_gnn_W_up1"])],
                       products, lambda b, ps, link: nc.vector.tensor_copy(rows[:, b, :], ps))
            with nc.semaphore("up_out") as stored, nc.Block() as block:
                @block.sync
                def _(sp):
                    sp.dma_start(tableU.rearrange("(b p) d -> p b d", p=BN), rows[:, :, :]).then_inc(stored, 16)
                    sp.wait_ge(stored, 16)
        message_pass(pg, "u", tableU, total)
        totalT = pg.sb("total2T", [P, 8, NODES], ctx=ctx)
        w_out = pg.sb("w_out", [P, 4, MUL], ctx=ctx)
        transpose_nodes(pg, "t3", total, totalT, 8)
        with nc.Block() as block:
            pass
        scale = SILU_2MOM / np.sqrt(float(HID)) / np.sqrt(float(MUL)) / np.sqrt(2.0 * MUL) / 10.0
        tmp = pg.sb("out_tmp", [BN, MUL], ctx=ctx)

        def products(b, ps):
            outs = [((0,), (0,)), ((2, 5), (2, 3)), ((3, 6), (2, 3)), ((4, 7), (2, 3))]
            for n, (blocks, ws) in enumerate(outs):
                accumulate(nc, ps[0:BN, n * MUL:(n + 1) * MUL],
                           [(totalT[:, f, nodes_of(b)], w_out[:, w, :]) for f, w in zip(blocks, ws)])
            return nc.tensor.matmul(p4_ps[b % 2][0:BN, 0:MUL], totalT[:, 1, nodes_of(b)], w_out[:, 1, :],
                                    start=True, stop=True)

        def finish(b, ps, link):
            link(nc.vector.scalar_tensor_tensor(out=pg.x[:, b, 0:MUL], in0=ps[:, 0:MUL], scalar=float(scale),
                                                in1=pg.x[:, b, 0:MUL], op0=ALU.mult, op1=ALU.add))
            link(nc.vector.scalar_tensor_tensor(out=pg.x[:, b, 0:MUL], in0=p4_ps[b % 2][0:BN, 0:MUL],
                                                scalar=float(scale / np.sqrt(3.0)), in1=pg.x[:, b, 0:MUL],
                                                op0=ALU.mult, op1=ALU.add))
            xv = pg.x[:, b, MUL:D].rearrange("p (u m) -> p m u", m=3)
            return nc.vector.scalar_tensor_tensor(out=xv, in0=ps[:, MUL:D].rearrange("p (m u) -> p m u", m=3),
                                                  scalar=float(scale), in1=xv, op0=ALU.mult, op1=ALU.add)

        with ExitStack() as banks:
            p4_ps = [banks.enter_context(nc.psum_tensor(f"p4_ps{n}", [P, D], FP32)) for n in range(2)]
            node_stage(pg, "out", [(w_out[:, 0:2, :], weight_rows(pg.inp["L2_gnn_W_out0"])),
                                   (w_out[:, 2:4, :], weight_rows(pg.inp["L2_gnn_W_out1"]))], products, finish)


def edge_mlp_pass(pg, table_src, by_dst, w_attr, w_attr_rest, w2, bias2, total):
    nc = pg.nc
    LAST = NG - 1

    def next_first(g, j, at):
        ahead, f = (1, j + 1) if j < 3 else (2, 0)
        return (g + ahead, ahead, f) if at + ahead <= LAST else None

    BUSY = RING * TG
    with ExitStack() as ctx:
        got = pg.sb("e_got", [P, 2 * TG, 2 * D], BF16, ctx)
        idx = pg.sb("e_idx", [P, 2, TG], U32, ctx)
        hot = pg.sb("e_hot", [P, RING * TG, BN], BF16, ctx)
        hotT = pg.sb("e_hotT", [BN, SG], BF16, ctx)
        dst_part = pg.sb("e_dst_part", [BN, 2, D], BF16, ctx)
        attrT = pg.sb("e_attrT", [P, 2, SG], BF16, ctx)
        first = pg.sb("e_first", [P, 2, 2, 4, SG], BF16, ctx)
        msg = pg.sb("e_msg", [P, 2, 2, D], BF16, ctx)
        act1 = pg.sb("e_act1", [P, 2, SG], ctx=ctx)
        act2 = pg.sb("e_act2", [P, 2, SG], ctx=ctx)
        mish1 = pg.sb("e_mish1", [P, 2, SG], ctx=ctx)
        mish2 = pg.sb("e_mish2", [P, 2, SG], ctx=ctx)
        lin2 = pg.sb("e_lin2", [P, 2, SG], ctx=ctx)
        hotT_ps = ctx.enter_context(nc.psum_tensor("e_hotT_ps", [P, 2 * SG], BF16))
        pre_ps = [ctx.enter_context(nc.psum_tensor(f"e_pre_ps{n}", [P, SG], FP32)) for n in range(2)]
        two_ps = [ctx.enter_context(nc.psum_tensor(f"e_two_ps{n}", [P, SG], FP32)) for n in range(2)]
        sum_ps = [ctx.enter_context(nc.psum_tensor(f"e_sum_ps{n}", [P, D], FP32)) for n in range(2)]
        sems = gather_sems(pg, ctx, "e")
        (cleared, hot_ready, hot_free, attr_free, hotT_turned, hotT_ready, dst_ready, pre_ready, act1_chain,
         act2_chain, den1_ready, den2_ready, clamped1, clamped2, mish1_ready, mish2_ready, split1, split2,
         first_done, two_biased, two_ready, msg_done, added) = (
            ctx.enter_context(nc.semaphore(f"e_{n}")) for n in (
                "cleared", "hot_ready", "hot_free", "attr_free", "hotT_turned", "hotT_ready", "dst_ready",
                "pre_ready", "act1_chain", "act2_chain", "den1_ready", "den2_ready", "clamped1", "clamped2",
                "mish1_ready", "mish2_ready", "split1", "split2", "first_done", "two_biased", "two_ready",
                "msg_done", "added"))
        attr_in = [ctx.enter_context(nc.semaphore(f"e_attr_in{h}")) for h in range(2)]
        block = ctx.enter_context(nc.Block())

        @block.sync
        def _(sp):
            sp.sem_inc(attr_free, 2)
            with sp.Fori(0, NG // 2) as i:
                for h in range(2):
                    sp.wait_ge(attr_free, 2 * i + h + 1)
                    for n, part in enumerate((pg.attrT, pg.attr_restT)):
                        sp.dma_start(attrT[n * HID:(n + 1) * HID, h, :],
                                     part[bass.ds(2 * i + h, 1), :, :].rearrange("a r e -> (a r) e"))\
                            .then_inc(attr_in[h], 16)

        @block.gpsimd
        def _(pool):
            idx_copied, passed = sems["idx_copied"], sems["passed"]

            def gather(g, h):
                pool.wait_ge(sems["gather_free"], (g + 1) * TG)
                pool.sem_inc(passed, 1)
                nc.gpsimd.tensor_copy(idx[:, h, :], pg.src_row[:, bass.ds(g * TG, TG)]).then_inc(idx_copied, 1)
                pool.wait_ge(idx_copied, g + 1)
                pool.sem_inc(passed, 1)
                for k in range(TG):
                    nc.gpsimd.indirect_dma_start(
                        out=got[:, h * TG + k, :], out_offset=None, in_=table_src,
                        in_offset=bass.IndirectOffsetOnAxis(ap=idx[:, h, k:k + 1], axis=0))\
                        .then_inc(sems["arrived"][h * TG + k], 16)

            def one(g, h, f):
                pool.wait_ge(split1, 4 * g + f + 1)
                nc.gpsimd.tensor_tensor(first[:, h, 1, f, :], mish1[:, f % 2, :], first[:, h, 0, f, :],
                                        ALU.subtract).then_inc(first_done, 1)

            def two(g, k):
                pool.wait_ge(split2, 4 * g + k + 1)
                nc.gpsimd.tensor_tensor(msg[:, k % 2, 1, :], mish2[:, k % 2, :], msg[:, k % 2, 0, :],
                                        ALU.subtract).then_inc(msg_done, 1)

            def body(g, r, at):
                for j in range(TG):
                    if ahead := next_first(g, j, at):
                        one(ahead[0], (r + ahead[1]) % 2, ahead[2])
                    two(g, j)
                    if j == 0 and at < LAST - 1:
                        gather(g + 2, r % 2)

            nc.gpsimd.memset(total[:, :, :], 0.0).then_inc(cleared, 1)
            pool.sem_inc(first_done, 2)
            pool.sem_inc(msg_done, 2)
            gather(0, 0)
            gather(1, 1)
            for f in range(4):
                one(0, 0, f)
            one(1, 1, 0)
            four_at_a_time(pool, body)

        @block.tensor
        def _(pe):
            def turn_hot(g, r):
                pe.wait_ge(hot_ready, (g + 1) * TG)
                for k in range(TG):
                    last = nc.tensor.transpose(hotT_ps[0:BN, k * P:(k + 1) * P], hot[:, r * TG + k, :],
                                               pg.ident16[:, :])
                last.then_inc(hotT_turned, 1)

            def first_layer(g, h, f):
                cols = slice(f * P, (f + 1) * P)
                pe.wait_ge(mish1_ready, 4 * g + f + 1)
                if f == 0:
                    pe.wait_ge(hotT_ready, g + 1)
                    pe.wait_ge(dst_ready, g + 1)
                    pe.wait_ge(attr_in[h], (g - h) * 16 + 32)
                    for k in range(TG):
                        b = h * TG + k
                        pe.wait_ge(sems["arrived"][b], sems["before"][b] + (g - h) * 8 + 16)
                ps = pre_ps[f % 2]
                nc.tensor.matmul(ps[:, :], dst_part[:, 0, cols], hotT[:, :], start=True, stop=False)
                nc.tensor.matmul(ps[:, :], dst_part[:, 1, cols], hotT[:, :], start=False, stop=False)
                nc.tensor.matmul(ps[:, :], w_attr[:, cols], attrT[:, h, :], start=False, stop=False)
                nc.tensor.matmul(ps[:, :], w_attr_rest[:, cols], attrT[0:HID, h, :], start=False, stop=False)
                for k in range(TG):
                    for part in range(2):
                        last = nc.tensor.matmul(ps[:, k * P:(k + 1) * P],
                                                got[:, h * TG + k, part * D + f * P:part * D + (f + 1) * P],
                                                pg.ident16[:, :], start=False, stop=(k == TG - 1 and part == 1))
                last.then_inc(pre_ready, 1)
                if f == 3:
                    pe.wait_ge(pre_ready, 4 * g + 4)
                    pe.sem_inc(attr_free, 1)
                    pe.sem_inc(sems["gather_free"], TG)

            def second_layer(g, h, k):
                pe.wait_ge(first_done, 4 * g + 4 + 2)
                pe.wait_ge(two_biased, 4 * g + k + 1)
                tile = slice(k * P, (k + 1) * P)
                pairs = []
                for f in range(4):
                    high, low = first[:, h, 0, f, tile], first[:, h, 1, f, tile]
                    pairs += [(high, w2[:, 0, f, :]), (high, w2[:, 1, f, :]), (low, w2[:, 0, f, :])]
                accumulate(nc, two_ps[k % 2][:, :], pairs).then_inc(two_ready, 1)

            def scatter(g, r, k):
                pe.wait_ge(msg_done, 4 * g + k + 3)
                if k == 0:
                    pe.wait_ge(added, g + 1)
                for part in range(2):
                    last = nc.tensor.matmul(sum_ps[r % 2][0:BN, :], hot[:, r * TG + k, :], msg[:, k % 2, part, :],
                                            start=(k == 0 and part == 0), stop=(k == TG - 1 and part == 1))
                last.then_inc(hot_free, 1)

            def body(g, r, at):
                for j in range(TG):
                    if j == 3 and at < LAST - 1:
                        turn_hot(g + 2, (r + 2) % RING)
                    second_layer(g, r % 2, j)
                    if ahead := next_first(g, j, at):
                        first_layer(ahead[0], (r + ahead[1]) % 2, ahead[2])
                    if j >= 2:
                        scatter(g, r, j - 2)
                    elif at > 0:
                        scatter(g - 1, (r - 1) % RING, j + 2)

            pe.sem_inc(hot_free, BUSY)
            turn_hot(0, 0)
            for f in range(4):
                first_layer(0, 0, f)
            turn_hot(1, 1)
            first_layer(1, 1, 0)
            four_at_a_time(pe, body)
            scatter(LAST, LAST % RING, 2)
            scatter(LAST, LAST % RING, 3)

        @block.scalar
        def _(act):
            def turned_one_hots(g):
                act.wait_ge(hotT_turned, g + 1)
                nc.scalar.copy(hotT[:, :], hotT_ps[0:BN, 0:SG]).then_inc(hotT_ready, 1)

            def mish_parts(*which):
                one_of, two_of = (clamped1, act1_chain, den1_ready, act1), (clamped2, act2_chain, den2_ready, act2)
                todo = [(4 * g + k, *(two_of if kind == "two" else one_of), k % 2) for kind, g, k in which]
                for n, clamped, chain, ready, act_buf, b in todo:
                    act.wait_ge(clamped, n + 1)
                    nc.scalar.activation(act_buf[:, b, :], act_buf[:, b, :], ACT.Exp).then_inc(chain, 1)
                for step, func in ((1, ACT.Square), (2, ACT.Ln)):
                    for n, clamped, chain, ready, act_buf, b in todo:
                        act.wait_ge(chain, 3 * n + step)
                        nc.scalar.activation(act_buf[:, b, :], act_buf[:, b, :], func,
                                             bias=pg.ones[:, 0:1]).then_inc(chain, 1)
                for n, clamped, chain, ready, act_buf, b in todo:
                    act.wait_ge(chain, 3 * n + 3)
                    nc.scalar.activation(act_buf[:, b, :], act_buf[:, b, :], ACT.Exp, scale=-1.0,
                                         bias=pg.ln2[:, 0:1]).then_inc(ready, 1)

            def body(g, r, at):
                for j in range(TG):
                    if j == 3 and at < LAST - 1:
                        turned_one_hots(g + 2)
                    if ahead := next_first(g, j, at):
                        mish_parts(("two", g, j), ("one", ahead[0], ahead[2]))
                    else:
                        mish_parts(("two", g, j))

            nc.scalar.preload_act_table_set("natural_log_exp_and_others")
            turned_one_hots(0)
            for f in range(4):
                mish_parts(("one", 0, f))
            turned_one_hots(1)
            mish_parts(("one", 1, 0))
            four_at_a_time(act, body)

        @block.vector
        def _(dve):
            def block_rows(g):
                at = nc.vector.value_load(pg.block_of_group[0:1, bass.ds(g, 1)], min_val=0, max_val=NB - 1)
                dve.wait_ge(hotT_turned, g + 1)
                nc.vector.tensor_copy(dst_part[:, :, :].rearrange("p a d -> p (a d)"),
                                      by_dst[:, bass.ds(at, 1), :, :].rearrange("p b a d -> p (b a d)"))\
                    .then_inc(dst_ready, 1)

            def clamp_one(g, f):
                dve.wait_ge(pre_ready, 4 * g + f + 1)
                nc.vector.tensor_scalar(act1[:, f % 2, :], pre_ps[f % 2][:, :], LIMIT, None, ALU.min)\
                    .then_inc(clamped1, 1)

            def one(g, f):
                n = 4 * g + f
                dve.wait_ge(den1_ready, n + 1)
                dve.wait_ge(first_done, n + 1)
                nc.vector.scalar_tensor_tensor(out=mish1[:, f % 2, :], in0=act1[:, f % 2, :], scalar=1.0,
                                               in1=pre_ps[f % 2][:, :], op0=ALU.subtract, op1=ALU.mult,
                                               reverse0=True).then_inc(mish1_ready, 1)

            def round_one(g, h, f):
                dve.wait_ge(mish1_ready, 4 * g + f + 3)
                nc.vector.tensor_copy(first[:, h, 0, f, :], mish1[:, f % 2, :]).then_inc(split1, 1)

            def clamp_two(g, k):
                n = 4 * g + k
                dve.wait_ge(two_ready, n + 1)
                nc.vector.tensor_tensor(lin2[:, k % 2, :], two_ps[k % 2][:, :], bias2[:, :], ALU.add)\
                    .then_inc(two_biased, 1)
                dve.wait_ge(two_biased, n + 3)
                nc.vector.tensor_scalar(act2[:, k % 2, :], lin2[:, k % 2, :], LIMIT, None, ALU.min)\
                    .then_inc(clamped2, 1)

            def two(g, k):
                n = 4 * g + k
                dve.wait_ge(den2_ready, n + 1)
                dve.wait_ge(msg_done, n + 1)
                nc.vector.scalar_tensor_tensor(out=mish2[:, k % 2, :], in0=act2[:, k % 2, :], scalar=1.0,
                                               in1=lin2[:, k % 2, :], op0=ALU.subtract, op1=ALU.mult,
                                               reverse0=True).then_inc(mish2_ready, 1)

            def round_two(g, k):
                n = 4 * g + k
                dve.wait_ge(mish2_ready, n + 3)
                dve.wait_ge(hot_free, n - 1 + BUSY)
                nc.vector.tensor_copy(msg[:, k % 2, 0, :], mish2[:, k % 2, :]).then_inc(split2, 1)

            def add(g, h):
                at = nc.vector.value_load(pg.block_of_group[0:1, bass.ds(g, 1)], min_val=0, max_val=NB - 1)
                dve.wait_ge(hot_free, (g + 1) * TG + BUSY)
                dve.wait_ge(added, g + 2)
                into = total[:, bass.ds(at, 1), :].rearrange("p a d -> p (a d)")
                nc.vector.tensor_tensor(into, into, sum_ps[h][0:BN, :], ALU.add).then_inc(added, 1)

            def clamps(g, j, at):
                clamp_two(g, j)
                if j == 3 and at < LAST - 1:
                    block_rows(g + 2)
                if ahead := next_first(g, j, at):
                    clamp_one(ahead[0], ahead[2])

            def body(g, r, at):
                for j in range(TG):
                    if j < 3:
                        clamps(g, j + 1, at)
                    elif at < LAST:
                        clamps(g + 1, 0, at + 1)
                    ahead = next_first(g, j, at)
                    if ahead:
                        one(ahead[0], ahead[2])
                    if ahead:
                        round_one(ahead[0], (r + ahead[1]) % 2, ahead[2])
                    two(g, j)
                    round_two(g, j)
                    if j == 2 and at > 0:
                        add(g - 1, (r - 1) % 2)
                    if j == 3 and at < LAST - 2:
                        hot_tiles(pg, dve, hot, hot_free, hot_ready, g + 3, (r + 3) % RING)

            dve.sem_inc(sems["gather_free"], 2 * TG)
            dve.sem_inc(added, 2)
            dve.sem_inc(mish1_ready, 2)
            dve.sem_inc(two_biased, 2)
            dve.sem_inc(mish2_ready, 2)
            for g in range(3):
                hot_tiles(pg, dve, hot, hot_free, hot_ready, g, g)
            dve.wait_ge(cleared, 1)
            block_rows(0)
            clamp_one(0, 0)
            for f in range(4):
                if f < 3:
                    clamp_one(0, f + 1)
                else:
                    block_rows(1)
                    clamp_one(1, 0)
                one(0, f)
                round_one(0, 0, f)
            clamps(0, 0, 0)
            one(1, 0)
            round_one(1, 1, 0)
            four_at_a_time(dve, body)
            add(LAST, LAST % 2)


def halve(pg, tag, jobs):
    nc = pg.nc
    with nc.semaphore(f"{tag}_halved") as halved, nc.Block() as block:
        @block.vector
        def _(dve):
            for n, (x, high, low) in enumerate(jobs):
                nc.vector.tensor_copy(high, x).then_inc(halved, 1)
            for n, (x, high, low) in enumerate(jobs):
                dve.wait_ge(halved, n + 1)
                nc.vector.tensor_tensor(low, x, high, ALU.subtract)


def layer3(pg):
    nc = pg.nc
    normalize(pg, "n3")
    table = nc.dram_tensor("src_table", [NODES, 2 * D], BF16).ap()
    w1 = pg.inp["L3_gnn_W1"]
    with ExitStack() as ctx:
        total = pg.sb("total3", [BN, NB, D], ctx=ctx)
        with ExitStack() as edges:
            by_dst = pg.sb("by_dst", [BN, NB, 2, D], BF16, edges)
            w_attr = pg.sb("w_attr", [P, D], BF16, edges)
            w_attr_rest = pg.sb("w_attr_rest", [HID, D], BF16, edges)
            w2 = pg.sb("w2", [P, 2, 4, D], BF16, edges)
            bias2 = pg.sb("bias2", [P, D], ctx=edges)
            with ExitStack() as early:
                w_src = pg.sb("w_src", [P, 4, D], ctx=early)
                w_dst = pg.sb("w_dst", [P, 4, D], ctx=early)
                bias1 = pg.sb("bias1", [BN, D], ctx=early)
                rows = pg.sb("src_rows", [BN, NB, 2, D], BF16, early)
                x_src = pg.sb("x_src", [BN, NB, D], ctx=early)
                x_dst = pg.sb("x_dst", [BN, NB, D], ctx=early)
                w_attr_f = pg.sb("w_attr_f", [P, D], ctx=early)
                w2_f = pg.sb("w2_f", [P, 4, D], ctx=early)
                unused = pg.sb("w_attr_low", [P, D], BF16, early)
                node_stage(pg, "ws", [(w_src[:, :, :], weight_rows(w1[0:D, :])),
                                      (w_attr_f[0:HID, :], w1[2 * D:2 * D + HID, :]),
                                      (w_attr_f[HID:P, :], w1[2 * D:2 * D + HID, :]),
                                      (w2_f[:, :, :], weight_rows(pg.inp["L3_gnn_W2"]))],
                           lambda b, ps: accumulate(nc, ps[0:BN, :], [(pg.hT[:, f, nodes_of(b)], w_src[:, f, :])
                                                                      for f in range(4)]),
                           lambda b, ps, link: nc.vector.tensor_copy(x_src[:, b, :], ps))
                halve(pg, "hs", [(x_src[:, b, :], rows[:, b, 0, :], rows[:, b, 1, :]) for b in range(NB)]
                      + [(w_attr_f[:, :], w_attr[:, :], unused[:, :])])
                with nc.semaphore("src_out") as stored, nc.Block() as block:
                    @block.sync
                    def _(sp):
                        sp.dma_start(table.rearrange("(b p) d -> p b d", p=BN),
                                     rows[:, :, :, :].rearrange("p b a d -> p b (a d)")).then_inc(stored, 16)
                        sp.wait_ge(stored, 16)
                node_stage(pg, "wd", [(w_dst[:, :, :], weight_rows(w1[D:2 * D, :])),
                                      (bias1[:, :], row_on_all(pg.inp["L3_gnn_b1"], BN)),
                                      (bias2[:, :], row_on_all(pg.inp["L3_gnn_b2"], P))],
                           lambda b, ps: accumulate(nc, ps[0:BN, :], [(pg.hT[:, f, nodes_of(b)], w_dst[:, f, :])
                                                                      for f in range(4)]),
                           lambda b, ps, link: nc.vector.tensor_tensor(x_dst[:, b, :], ps, bias1[:, :], ALU.add))
                halve(pg, "hd", [(x_dst[:, b, :], by_dst[:, b, 0, :], by_dst[:, b, 1, :]) for b in range(NB)]
                      + [(w2_f[:, f, :], w2[:, 0, f, :], w2[:, 1, f, :]) for f in range(4)]
                      + [(w_attr_f[0:HID, :], w_attr[0:HID, :], w_attr_rest[:, :])])
            edge_mlp_pass(pg, table, by_dst, w_attr, w_attr_rest, w2, bias2, total)
        totalT = pg.sb("total3T", [P, 4, NODES], ctx=ctx)
        transpose_nodes(pg, "t4", total, totalT, 4)
        w3 = pg.sb("w3", [P, 8, D], ctx=ctx)
        w4 = pg.sb("w4", [P, 4, D], ctx=ctx)
        rows = {n: pg.sb(f"{n}_row", [BN, D], ctx=ctx) for n in ("b3", "b4", "gamma", "beta")}
        u = pg.sb("u_nodes", [BN, NB, D], ctx=ctx)
        e = pg.sb("e_nodes", [BN, NB, D], ctx=ctx)
        node_stage(pg, "w3s", [(w3[:, :, :], weight_rows(pg.inp["L3_gnn_W3"])),
                               (rows["b3"][:, :], row_on_all(pg.inp["L3_gnn_b3"], BN))],
                   lambda b, ps: accumulate(nc, ps[0:BN, :],
                                            [(pg.hT[:, f, nodes_of(b)], w3[:, f, :]) for f in range(4)]
                                            + [(totalT[:, f, nodes_of(b)], w3[:, 4 + f, :]) for f in range(4)]),
                   lambda b, ps, link: nc.vector.tensor_tensor(u[:, b, :], ps, rows["b3"][:, :], ALU.add))
        with nc.semaphore("mish_act") as acts, nc.semaphore("mish_dve") as dves, nc.Block() as block:
            @block.scalar
            def _(act):
                act.wait_ge(dves, 1)
                nc.scalar.activation(e[:, :, :], e[:, :, :], ACT.Exp).then_inc(acts, 1)
                act.wait_ge(acts, 1)
                nc.scalar.activation(e[:, :, :], e[:, :, :], ACT.Square, bias=pg.ones[0:BN, 0:1]).then_inc(acts, 1)
                act.wait_ge(acts, 2)
                nc.scalar.activation(e[:, :, :], e[:, :, :], ACT.Ln, bias=pg.ones[0:BN, 0:1]).then_inc(acts, 1)
                act.wait_ge(acts, 3)
                nc.scalar.activation(e[:, :, :], e[:, :, :], ACT.Exp, scale=-1.0,
                                     bias=pg.ln2[0:BN, 0:1]).then_inc(acts, 1)

            @block.vector
            def _(dve):
                nc.vector.tensor_scalar(e[:, :, :], u[:, :, :], LIMIT, None, ALU.min).then_inc(dves, 1)
                dve.wait_ge(acts, 4)
                nc.vector.scalar_tensor_tensor(out=u[:, :, :], in0=e[:, :, :], scalar=1.0, in1=u[:, :, :],
                                               op0=ALU.subtract, op1=ALU.mult, reverse0=True)
        transpose_nodes(pg, "t5", u, totalT, 4)

        def finish(b, ps, link):
            link(nc.vector.tensor_tensor(e[:, b, :], pg.h[:, b, :], ps, ALU.add))
            return nc.vector.tensor_tensor(e[:, b, :], e[:, b, :], rows["b4"][:, :], ALU.add)

        node_stage(pg, "w4s", [(w4[:, :, :], weight_rows(pg.inp["L3_gnn_W4"]))]
                   + [(rows[n][:, :], row_on_all(pg.inp[f"L3_gnn_{n}"], BN)) for n in ("b4", "gamma", "beta")],
                   lambda b, ps: accumulate(nc, ps[0:BN, :], [(totalT[:, f, nodes_of(b)], w4[:, f, :])
                                                              for f in range(4)]), finish)
        stats = pg.sb("f_stats", [BN, NB, 6], ctx=ctx)
        mv = pg.sb("f_mv", [BN, NB, 2], ctx=ctx)
        sd = pg.sb("f_sd", [BN, NB], ctx=ctx)
        rs = pg.sb("f_rs", [BN, NB], ctx=ctx)
        with ExitStack() as sems:
            chain, var, root, final, stored = (sems.enter_context(nc.semaphore(f"f_{n}"))
                                               for n in ("chain", "var", "root", "final", "stored"))
            block = sems.enter_context(nc.Block())

            @block.scalar
            def _(act):
                act.wait_ge(var, 1)
                nc.scalar.sqrt(sd[:, :], sd[:, :]).then_inc(root, 1)

            @block.vector
            def _(dve):
                done = [0]

                def link(ins):
                    done[0] += 1
                    ins.then_inc(chain, 1)
                    dve.wait_ge(chain, done[0])

                for b in range(NB):
                    last = nc.vector.bn_stats(out=stats[:, b, :], in_=e[:, b, :])
                link(last)
                for b in range(NB):
                    last = nc.vector.bn_aggr(out=mv[:, b, :], in_=stats[:, b, :])
                link(last)
                nc.vector.tensor_scalar(sd[:, :], mv[:, :, 1], EPS, None, ALU.add).then_inc(var, 1)
                dve.wait_ge(root, 1)
                link(nc.vector.reciprocal(rs[:, :], sd[:, :]))
                for b in range(NB):
                    link(nc.vector.tensor_scalar(e[:, b, :], e[:, b, :], mv[:, b, 0:1], rs[:, b:b + 1],
                                                 ALU.subtract, ALU.mult))
                    link(nc.vector.tensor_tensor(e[:, b, :], e[:, b, :], rows["gamma"][:, :], ALU.mult))
                    link(nc.vector.tensor_tensor(e[:, b, :], e[:, b, :], rows["beta"][:, :], ALU.add))
                    nc.vector.tensor_tensor(pg.x[:, b, :], pg.x[:, b, :], e[:, b, :], ALU.add).then_inc(final, 1)

            @block.sync
            def _(sp):
                for b in range(NB):
                    sp.wait_ge(final, b + 1)
                    sp.dma_start(pg.out[nodes_of(b), :], pg.x[:, b, :]).then_inc(stored, 16)
                sp.wait_ge(stored, 16 * NB)


STAGES = [constants, place_edges, order_edges, fetch_records, load_nodes, layer0, layer1, layer2, layer3]


OUT_SHAPE = (NODES, D)


def build(nc, args, out):
    pg = Program(nc, args, out)
    with pg.keep:
        for stage in STAGES:
            stage(pg)
            nc.all_engine_barrier(sems_to_clear=range(pg.arrived[-1].num + 1, max(nc.free_semaphores) + 1))


def kernel(**inputs):
    import concourse.bacc as bacc
    from concourse.bass_utils import run_bass_kernel_spmd

    data = {name: np.asarray(a) for name, a in inputs.items()}
    data["edge_floats"] = np.concatenate(
        [data.pop("edge_attr_64"), data.pop("edge_attr_8"), data.pop("edge_attr_4"),
         data.pop("edge_weight")[:, None], np.zeros((EDGES, RECORD - SRC), np.float32)], axis=1)
    data["L0_gnn_W"] = data["L0_gnn_W"].T

    nc = bacc.Bacc("TRN2", target_bir_lowering=False, num_devices=1)
    arrays, args = {}, {}
    for name, a in data.items():
        a = np.ascontiguousarray(a)
        arrays[f"in_{name}_dram"] = a
        args[name] = nc.dram_tensor(f"in_{name}_dram", a.shape, mybir.dt.from_np(a.dtype), kind="ExternalInput").ap()
    out = nc.dram_tensor("out_0_dram", OUT_SHAPE, FP32, kind="ExternalOutput").ap()
    build(nc, args, out)
    result = run_bass_kernel_spmd(nc, [arrays], core_ids=[0])
    return result.results[0]["out_0_dram"]
```
